# Optimizing a Trainium2 kernel written in Bass

```python
import numpy as np
import jax
import jax.numpy as jnp

def _softmax(x, axis=-1):
    return jax.nn.softmax(x, axis=axis)

def _gelu(x):
    return jax.nn.gelu(x, approximate=True)

def _silu(x):
    return jax.nn.silu(x)

def _sigmoid(x):
    return jax.nn.sigmoid(x)

def _layernorm(x, axis=-1, eps=1e-05):
    m = jnp.mean(x, axis=axis, keepdims=True)
    v = jnp.var(x, axis=axis, keepdims=True)
    return (x - m) / jnp.sqrt(v + eps)

def _scatter_add(tgt, idx, src, axis=0):
    return tgt.at[idx].add(src)

def _segment_sum(src, seg, n):
    return jax.ops.segment_sum(src, seg, n)
kernel_name = 'mk_seq_postln_d1_jaxref_r4_790da4'

def setup_inputs(seed: int=0):
    np.random.seed(seed)
    _w = jnp.asarray

    def _L0_attn_setup():
        import jax, jax.numpy as jnp
        import numpy as np
        from jax import lax
        DIM = 256
        DS = 16
        DC = 4
        EXP = 2
        DI = DIM * EXP
        B, L = (2, 256)

        def _ssm(x, x_proj_w, dt_w, dt_b, A_log, D_skip):
            xp = jnp.einsum('bli,pi->blp', x, x_proj_w)
            delta = jax.nn.softplus(xp[..., :1] * dt_w[:, 0] + dt_b)
            Bp = xp[..., 1:DS + 1]
            Cp = xp[..., DS + 1:]
            A = -jnp.exp(A_log)
            dA = jnp.exp(delta[..., None] * A)
            dB = delta[..., None] * Bp[:, :, None, :] * x[..., None]

            def step(h, inp):
                dA_t, dB_t, C_t = inp
                h = dA_t * h + dB_t
                return (h, jnp.einsum('bdn,bn->bd', h, C_t))
            h0 = jnp.zeros((x.shape[0], DI, DS), x.dtype)
            _, ys = lax.scan(step, h0, (jnp.swapaxes(dA, 0, 1), jnp.swapaxes(dB, 0, 1), jnp.swapaxes(Cp, 0, 1)))
            y = jnp.swapaxes(ys, 0, 1)
            return y + x * D_skip
        key = jax.random.key(seed)
        ks = jax.random.split(key, 10)
        s = lambda k, shape, sc: jax.random.normal(k, shape, jnp.float32) * sc
        return {'x': s(ks[0], (B, L, DIM), 1.0), 'norm_w': jnp.ones((DIM,), jnp.float32), 'norm_b': jnp.zeros((DIM,), jnp.float32), 'in_proj_w': s(ks[1], (2 * DI, DIM), DIM ** (-0.5)), 'conv_w': s(ks[2], (DI, 1, DC), DC ** (-0.5)), 'conv_b': jnp.zeros((DI,), jnp.float32), 'x_proj_w': s(ks[3], (2 * DS + 1, DI), DI ** (-0.5)), 'dt_w': s(ks[4], (DI, 1), 1.0), 'dt_b': jax.random.uniform(ks[5], (DI,), jnp.float32, -0.001, 0.001), 'A_log': s(ks[6], (DI, DS), 1.0), 'D_skip': jnp.ones((DI,), jnp.float32), 'out_proj_w': s(ks[7], (DIM, DI), DI ** (-0.5))}
    _L0_attn_in = _L0_attn_setup()

    def _L0_ffn_setup():
        import math
        import jax, jax.numpy as jnp
        import numpy as np
        D_MODEL = 256
        D_HIDDEN = 1024
        N_EXPERTS = 8
        TOP_K = 2
        CAPACITY_FACTOR = 1.25
        key = jax.random.key(seed)
        ks = jax.random.split(key, 8)
        s = 0.02
        x = jax.random.normal(ks[0], (4, 512, D_MODEL), dtype=jnp.float32)
        router_w = jax.random.normal(ks[1], (D_MODEL, N_EXPERTS), dtype=jnp.float32) * s
        router_b = jnp.zeros((N_EXPERTS,), dtype=jnp.float32)
        w1 = jax.random.normal(ks[2], (N_EXPERTS, D_MODEL, D_HIDDEN), dtype=jnp.float32) * s
        b1 = jnp.zeros((N_EXPERTS, D_HIDDEN), dtype=jnp.float32)
        w2 = jax.random.normal(ks[3], (N_EXPERTS, D_HIDDEN, D_MODEL), dtype=jnp.float32) * s
        b2 = jnp.zeros((N_EXPERTS, D_MODEL), dtype=jnp.float32)
        return {'x': x, 'router_w': router_w, 'router_b': router_b, 'w1': w1, 'b1': b1, 'w2': w2, 'b2': b2}
    _L0_ffn_in = _L0_ffn_setup()
    _d = {'L0_attn_x': _L0_attn_in['x'], 'L0_attn_norm_w': _L0_attn_in['norm_w'], 'L0_attn_norm_b': _L0_attn_in['norm_b'], 'L0_attn_in_proj_w': _L0_attn_in['in_proj_w'], 'L0_attn_conv_w': _L0_attn_in['conv_w'], 'L0_attn_conv_b': _L0_attn_in['conv_b'], 'L0_attn_x_proj_w': _L0_attn_in['x_proj_w'], 'L0_attn_dt_w': _L0_attn_in['dt_w'], 'L0_attn_dt_b': _L0_attn_in['dt_b'], 'L0_attn_A_log': _L0_attn_in['A_log'], 'L0_attn_D_skip': _L0_attn_in['D_skip'], 'L0_attn_out_proj_w': _L0_attn_in['out_proj_w'], 'L0_ffn_router_w': _L0_ffn_in['router_w'], 'L0_ffn_router_b': _L0_ffn_in['router_b'], 'L0_ffn_w1': _L0_ffn_in['w1'], 'L0_ffn_b1': _L0_ffn_in['b1'], 'L0_ffn_w2': _L0_ffn_in['w2'], 'L0_ffn_b2': _L0_ffn_in['b2']}
    _x0 = _d['L0_attn_x']
    _d['L0_attn_x'] = jax.random.normal(jax.random.fold_in(jax.random.key(seed), 1), (2, 2048, 256), dtype=_x0.dtype)
    del _x0
    return _d

def reference(L0_attn_x, L0_attn_norm_w, L0_attn_norm_b, L0_attn_in_proj_w, L0_attn_conv_w, L0_attn_conv_b, L0_attn_x_proj_w, L0_attn_dt_w, L0_attn_dt_b, L0_attn_A_log, L0_attn_D_skip, L0_attn_out_proj_w, L0_ffn_router_w, L0_ffn_router_b, L0_ffn_w1, L0_ffn_b1, L0_ffn_w2, L0_ffn_b2):

    def _L0_attn_ref(x, norm_w, norm_b, in_proj_w, conv_w, conv_b, x_proj_w, dt_w, dt_b, A_log, D_skip, out_proj_w):
        import jax, jax.numpy as jnp
        import numpy as np
        from jax import lax
        DIM = 256
        DS = 16
        DC = 4
        EXP = 2
        DI = DIM * EXP
        B, L = (2, 256)

        def _ssm(x, x_proj_w, dt_w, dt_b, A_log, D_skip):
            xp = jnp.einsum('bli,pi->blp', x, x_proj_w)
            delta = jax.nn.softplus(xp[..., :1] * dt_w[:, 0] + dt_b)
            Bp = xp[..., 1:DS + 1]
            Cp = xp[..., DS + 1:]
            A = -jnp.exp(A_log)
            dA = jnp.exp(delta[..., None] * A)
            dB = delta[..., None] * Bp[:, :, None, :] * x[..., None]

            def step(h, inp):
                dA_t, dB_t, C_t = inp
                h = dA_t * h + dB_t
                return (h, jnp.einsum('bdn,bn->bd', h, C_t))
            h0 = jnp.zeros((x.shape[0], DI, DS), x.dtype)
            _, ys = lax.scan(step, h0, (jnp.swapaxes(dA, 0, 1), jnp.swapaxes(dB, 0, 1), jnp.swapaxes(Cp, 0, 1)))
            y = jnp.swapaxes(ys, 0, 1)
            return y + x * D_skip
        mu = x.mean(-1, keepdims=True)
        var = ((x - mu) ** 2).mean(-1, keepdims=True)
        xn = (x - mu) * lax.rsqrt(var + 1e-05) * norm_w + norm_b
        xz = jnp.einsum('bld,pd->blp', xn, in_proj_w)
        xi, z = (xz[..., :DI], xz[..., DI:])
        xc = lax.conv_general_dilated(jnp.swapaxes(xi, 1, 2), conv_w, (1,), [(DC - 1, 0)], feature_group_count=DI, dimension_numbers=('NCH', 'OIH', 'NCH'))
        xc = jnp.swapaxes(xc + conv_b[None, :, None], 1, 2)
        xc = jax.nn.silu(xc)
        y = _ssm(xc, x_proj_w, dt_w, dt_b, A_log, D_skip)
        y = y * jax.nn.silu(z)
        return x + jnp.einsum('bli,di->bld', y, out_proj_w)

    def _L0_ffn_ref(x, router_w, router_b, w1, b1, w2, b2):
        import math
        import jax, jax.numpy as jnp
        import numpy as np
        D_MODEL = 256
        D_HIDDEN = 1024
        N_EXPERTS = 8
        TOP_K = 2
        CAPACITY_FACTOR = 1.25
        B, T, D = x.shape
        N = B * T
        E = N_EXPERTS
        capacity = max(1, math.ceil(N / E * CAPACITY_FACTOR))
        x_flat = x.reshape(N, D)
        logits = x_flat.astype(jnp.float32) @ router_w + router_b
        gates = jax.nn.softmax(logits, axis=-1)
        _, topk_idx = jax.lax.top_k(gates, TOP_K)
        expert_mask = jax.nn.one_hot(topk_idx, E, dtype=jnp.int32).sum(1)
        pos = jnp.cumsum(expert_mask, axis=0) - 1
        expert_mask = expert_mask * (pos < capacity)
        valid = expert_mask > 0
        pos_c = jnp.where(valid, pos, capacity)
        e_idx = jnp.broadcast_to(jnp.arange(E), (N, E))
        dispatched = x_flat[:, None, :] * valid[:, :, None].astype(x.dtype)
        buf = jnp.zeros((E, capacity + 1, D), x.dtype).at[e_idx.ravel(), pos_c.ravel()].add(dispatched.reshape(N * E, D))
        buf = buf[:, :capacity]
        h = jax.nn.gelu(jnp.einsum('ecd,edh->ech', buf, w1) + b1[:, None, :], approximate=False)
        out = jnp.einsum('ech,ehd->ecd', h, w2) + b2[:, None, :]
        pos_g = jnp.minimum(pos_c, capacity - 1)
        gathered = out[e_idx, pos_g]
        weights = (gates * valid).astype(x.dtype)
        y = jnp.einsum('ned,ne->nd', gathered, weights)
        return y.reshape(B, T, D)
    x = L0_attn_x
    x = _layernorm(x + _L0_attn_ref(x, L0_attn_norm_w, L0_attn_norm_b, L0_attn_in_proj_w, L0_attn_conv_w, L0_attn_conv_b, L0_attn_x_proj_w, L0_attn_dt_w, L0_attn_dt_b, L0_attn_A_log, L0_attn_D_skip, L0_attn_out_proj_w), axis=-1)
    x = _layernorm(x + _L0_ffn_ref(x, L0_ffn_router_w, L0_ffn_router_b, L0_ffn_w1, L0_ffn_b1, L0_ffn_w2, L0_ffn_b2), axis=-1)
    return x

_drawn_inputs = setup_inputs


def setup_inputs(seed=0):
    import zlib

    import numpy as np

    out = dict(_drawn_inputs(seed))
    spreads = {'L0_attn_norm_w': (1.0, 0.2),
     'L0_attn_norm_b': (0.0, 0.1),
     'L0_attn_conv_b': (0.0, 0.1),
     'L0_attn_D_skip': (1.0, 0.2),
     'L0_ffn_router_b': (0.0, 0.476),
     'L0_ffn_b1': (0.0, 0.8),
     'L0_ffn_b2': (0.0, 0.4)}
    factors = {'L0_attn_dt_b': 200.0}
    for name, (base, spread) in spreads.items():
        noise = np.random.default_rng([zlib.crc32(name.encode()), seed]).standard_normal(out[name].shape)
        drawn = base * np.exp(spread * noise) if base else spread * noise
        out[name] = jnp.asarray(drawn.astype(out[name].dtype))
    for name, factor in factors.items():
        out[name] = (out[name] * factor).astype(out[name].dtype)
    return out
```

```python
from contextlib import ExitStack

import concourse.bass as bass
from concourse import mybir

F32 = mybir.dt.float32
BF16 = mybir.dt.bfloat16
U32 = mybir.dt.uint32
ALU = mybir.AluOpType
ACT = mybir.ActivationFunctionType

P = 128
DIM = 256
DI = 512
DG = DI // P
KD = DIM // P
NST = 16
TAPS = 4
BATCH, SEQ = 2, 2048
TOK = BATCH * SEQ
NT = TOK // P
SEC = 512
QT = SEC // P
NB = NST // QT
STEPS = NB * DG
TPB = SEQ // P
XR = 12
EXPERTS, HID, CAP = 8, 1024, 640
SLOTS = EXPERTS * CAP
ST = CAP // P
HG = HID // P
HALF = CAP // 2
ROW = DIM + 2
EPS = 1e-5
FAR = 1.0e6
LEAD = QT
FT = 4

SCAN0 = STEPS
U0 = STEPS
HT0 = 4
ACC0 = 4
CARRY0 = NST
ACCZ0 = QT
GEL0 = 2
EOB0 = 2


def past(n):
    return n + 1


def build(nc, x, norm_w, norm_b, in_w, conv_w, conv_b, xp_w, dt_w, dt_b, a_log, d_skip, out_w,
          router_w, router_b, w1, b1, w2, b2, out):
    with ExitStack() as ctx:
        scope = [ctx]

        def sb(name, shape, dt=F32):
            return scope[0].enter_context(nc.sbuf_tensor(name, shape, dt))

        def sem(name):
            return ctx.enter_context(nc.semaphore(name))

        b_rows = nc.dram_tensor("b_rows", [NT // QT, NST, SEC], F32, kind="Internal").ap()
        slot_rows = nc.dram_tensor("slot_rows", [SLOTS, ROW], F32, kind="Internal").ap()
        y_rows = nc.dram_tensor("y_rows", [TOK, DIM], F32, kind="Internal").ap()

        banks = ctx.enter_context(nc.psum_tensor("banks", [P, 8, 512], F32))
        decay_ps = [banks[:, 0, :], banks[:, 1, :]]
        hT_ps = [banks[:, 2, :], banks[:, 3, :]]
        front_a, front_b = banks[:, 4, :], banks[:, 5, :]
        back_a, back_b = banks[:, 6, :], banks[:, 7, :]

        ident = sb("ident", [P, P])
        w1_sb = [sb("w1_even", [P, KD, HID])]
        w2_sb = [sb("w2_even", [P, HG, DIM])]
        b1_sb = sb("b1_sb", [P, EXPERTS, HG])
        mhalf = sb("mhalf", [P, FT])
        stat = sb("stat", [P, FT, 6])
        mv = sb("mv", [P, FT, 2])
        veps = sb("veps", [P, FT])
        rstd = sb("rstd", [P, FT])

        ssm = ExitStack()
        scope[0] = ssm
        in_sb = sb("in_sb", [P, KD, 2 * DI])
        out_sb = sb("out_sb", [P, DG, DIM])
        xp_sb = sb("xp_sb", [P, DG, 1 + 2 * NST])
        rw_sb = sb("rw_sb", [P, KD, EXPERTS])
        rb_sb = sb("rb_sb", [P, EXPERTS])
        nw_sb = sb("nw_sb", [P, KD])
        nb_sb = sb("nb_sb", [P, KD])
        cw_sb = sb("cw_sb", [P, DG, TAPS])
        cb_sb = sb("cb_sb", [P, DG])
        ds_sb = sb("ds_sb", [P, DG])
        dt_sb = sb("dt_sb", [2, DI])
        alog_sb = sb("alog_sb", [P, DG, NST])
        aexp = sb("aexp", [P, DG, NST])
        nega = sb("nega", [P, NST, DG])
        conv_diag = sb("conv_diag", [P, DG, TAPS, P])
        skip_diag = sb("skip_diag", [P, DG, P])
        ones = sb("ones", [P, P])
        zero = sb("zero", [P, 1])
        ones_b = sb("ones_b", [P, P], BF16)
        upper = sb("upper", [P, P])
        upper_b = sb("upper_b", [P, P], BF16)
        iota8 = sb("iota8", [P, EXPERTS])
        token_no = sb("token_no", [P, NT])
        empty_row = sb("empty_row", [P, ROW])

        x_ring = sb("x_ring", [P, XR, DIM])
        xn = sb("xn", [P, DIM])
        xnT = sb("xnT", [P, KD, P])
        xi = sb("xi", [P, DG, TAPS - 1 + P])
        halo = sb("halo", [P, BATCH, DG, TAPS - 1])
        xc_tile = sb("xc_tile", [P, DG, P])
        xc = sb("xc", [P, 2, DG, SEC])
        sz = sb("sz", [P, 2, DG, SEC])
        bt_tile = sb("bt_tile", [1 + NST, P])
        xp0 = sb("xp0", [2, P])
        c_sb = sb("c_sb", [P, 2, QT, NST])
        sp_abs = sb("sp_abs", [P, DG, P])
        sp_exp = sb("sp_exp", [P, DG, P])
        sp_ln = sb("sp_ln", [P, DG, P])
        sp_relu = sb("sp_relu", [P, DG, P])
        delta = sb("delta", [P, 2, DG, SEC])
        dx = sb("dx", [P, 2, DG, SEC])
        b_bc = sb("b_bc", [P, 2, NB, SEC])
        u = sb("u", [P, 4, SEC])
        h = sb("h", [P, 2, DG, SEC])
        carry = sb("carry", [P, BATCH, NST, DG])
        acc = sb("acc", [P, 2, QT, DI])
        acc_tile = sb("acc_tile", [P, DI])
        y_tile = sb("y_tile", [P, DG, P])
        r_tile = sb("r_tile", [P, DIM])
        stat2 = sb("stat2", [P, 6])
        mv2 = sb("mv2", [P, 2])
        veps2 = sb("veps2", [P, 1])
        rstd2 = sb("rstd2", [P, 1])
        rows = sb("rows", [P, 2, ROW])
        x1T = sb("x1T", [P, KD, P])
        logits = sb("logits", [P, EXPERTS])
        top8 = sb("top8", [P, 8])
        idx8 = sb("idx8", [P, 8], U32)
        idxf = sb("idxf", [P, 2])
        choice = sb("choice", [P, 2, EXPERTS])
        mask_b = sb("mask_b", [P, EXPERTS], BF16)
        negmax = sb("negmax", [P, 1])
        gexp = sb("gexp", [P, EXPERTS])
        gden = sb("gden", [P, 1])
        gtop = sb("gtop", [P, 2])
        grec = sb("grec", [P, 1])
        taken = sb("taken", [P, EXPERTS])
        pos = sb("pos", [P, EXPERTS])
        pick = sb("pick", [P, 2, EXPERTS])
        posk = sb("posk", [P, 2])
        slotf = sb("slotf", [P, 2])
        over = sb("over", [P, 2])
        slot = sb("slot", [P, 2], U32)
        ssm.close()

        ffn = ExitStack()
        ctx.enter_context(ffn)
        scope[0] = ffn
        w1_sb.append(sb("w1_odd", [P, KD, HID]))
        w2_sb.append(sb("w2_odd", [P, HG, DIM]))
        xg = sb("xg", [P, 2, ST, ROW])
        gidx = sb("gidx", [P, 2, ST], U32)
        xgT = sb("xgT", [P, 2, KD, CAP])
        hid = sb("hid", [P, HG, CAP])
        b2_bc = sb("b2_bc", [P, EXPERTS, DIM])
        eo = sb("eo", [P, ST, DIM])
        eo_w = sb("eo_w", [P, 2, ST, DIM])
        yt = sb("yt", [P, 2, FT, DIM])
        yo = sb("yo", [P, 2, FT, DIM])
        rstd2x = sb("rstd2x", [P, 2, FT])
        nmr = sb("nmr", [P, 2, FT])

        weights_in = sem("weights_in")
        small_in = sem("small_in")
        x_loaded = sem("x_loaded")
        masks_made = sem("masks_made")
        consts_made = sem("consts_made")
        empty_made = sem("empty_made")
        state_zeroed = sem("state_zeroed")
        aexp_done = sem("aexp_done")
        nega_done = sem("nega_done")
        st1_done = sem("st1_done")
        mv1_done = sem("mv1_done")
        veps1_done = sem("veps1_done")
        rstd1_done = sem("rstd1_done")
        xn_done = sem("xn_done")
        xnT_psum = sem("xnT_psum")
        xnT_done = sem("xnT_done")
        xi_psum = sem("xi_psum")
        z_psum = sem("z_psum")
        halo_in = sem("halo_in")
        xi_done = sem("xi_done")
        conv_psum = sem("conv_psum")
        sz_done = sem("sz_done")
        xct_done = sem("xct_done")
        xc_done = sem("xc_done")
        xp_psum = sem("xp_psum")
        xp_done = sem("xp_done")
        b_stored = sem("b_stored")
        b_loaded = sem("b_loaded")
        dt_psum = sem("dt_psum")
        spabs_done = sem("spabs_done")
        spexp_done = sem("spexp_done")
        spln_done = sem("spln_done")
        sprelu_done = sem("sprelu_done")
        delta_done = sem("delta_done")
        dx_done = sem("dx_done")
        u_ready = sem("u_ready")
        decay_ready = sem("decay_ready")
        scans_done = sem("scans_done")
        carry_saved = sem("carry_saved")
        hT_psum = sem("hT_psum")
        acc_done = sem("acc_done")
        acct_done = sem("acct_done")
        acc_zeroed = sem("acc_zeroed")
        yT_psum = sem("yT_psum")
        y_done = sem("y_done")
        o_psum = sem("o_psum")
        r_done = sem("r_done")
        st2_done = sem("st2_done")
        mv2_done = sem("mv2_done")
        veps2_done = sem("veps2_done")
        rstd2_done = sem("rstd2_done")
        x1_done = sem("x1_done")
        x1_copied = sem("x1_copied")
        y_stored = sem("y_stored")
        ids_done = sem("ids_done")
        x1T_psum = sem("x1T_psum")
        x1T_done = sem("x1T_done")
        lg_psum = sem("lg_psum")
        lg_done = sem("lg_done")
        top_done = sem("top_done")
        idx_done = sem("idx_done")
        idxf_done = sem("idxf_done")
        choice_done = sem("choice_done")
        mask_done = sem("mask_done")
        negmax_done = sem("negmax_done")
        gexp_done = sem("gexp_done")
        grec_done = sem("grec_done")
        gate_done = sem("gate_done")
        cnt_psum = sem("cnt_psum")
        pos_done = sem("pos_done")
        taken_done = sem("taken_done")
        pick_done = sem("pick_done")
        slotf_done = sem("slotf_done")
        over_done = sem("over_done")
        slot_done = sem("slot_done")
        scattered = sem("scattered")
        gidx_done = sem("gidx_done")
        xgT_psum = sem("xgT_psum")
        xgT_done = sem("xgT_done")
        up_psum = sem("up_psum")
        gelu_done = sem("gelu_done")
        down_psum = sem("down_psum")
        eob_done = sem("eob_done")
        eow_done = sem("eow_done")
        added = sem("added")
        landed = sem("landed")
        fst_done = sem("fst_done")
        fmv_done = sem("fmv_done")
        fveps_done = sem("fveps_done")
        frstd_done = sem("frstd_done")
        fo_done = sem("fo_done")
        fr_copied = sem("fr_copied")
        fnmr_done = sem("fnmr_done")
        w_in = [sem("w_in_even"), sem("w_in_odd")]
        xg_in = [sem("xg_in_even"), sem("xg_in_odd")]
        yt_in = [sem("yt_in_even"), sem("yt_in_odd")]
        out_st = [sem("out_st_even"), sem("out_st_odd")]

        def apart(eng):
            eng.nop(nofuse=True)

        PHASES = [(0, LEAD, True, False, False), (LEAD, 2 * LEAD, True, True, False),
                  (2 * LEAD, NT, True, True, True), (NT, NT + LEAD, False, True, True),
                  (NT + LEAD, NT + 2 * LEAD, False, False, True)]

        def tcol(t):
            return bass.ds((t % QT) * P, P)

        block = ctx.enter_context(nc.Block())

        @block.sync
        def _(sp):
            def load_expert(e, k):
                sp.dma_start(w1_sb[k][:, :, :], w1[e].rearrange("(k p) n -> p k n", p=P)).then_inc(w_in[k], 16)
                sp.dma_start(w2_sb[k][:, :, :], w2[e].rearrange("(g p) n -> p g n", p=P)).then_inc(w_in[k], 16)

            sp.dma_start(in_sb[:, :, :], in_w.rearrange("(k p) n -> p k n", p=P)).then_inc(weights_in, 16)
            sp.dma_start(x_ring[:, 0, :], x[0:P, :]).then_inc(x_loaded, 16)
            for dst, src in ((nw_sb[:, :], norm_w),
                             (nb_sb[:, :], norm_b),
                             (cw_sb[:, :, :], conv_w.rearrange("(g p) o j -> p g (o j)", p=P)),
                             (cb_sb[:, :], conv_b),
                             (ds_sb[:, :], d_skip),
                             (dt_sb[0:1, :], dt_w),
                             (dt_sb[1:2, :], dt_b.rearrange("(o d) -> o d", o=1)),
                             (alog_sb[:, :, :], a_log.rearrange("(g p) n -> p g n", p=P)),
                             (b1_sb[:, :, :], b1),
                             (rb_sb[:, :], router_b.partition_broadcast(P))):
                sp.dma_start(dst, src).then_inc(small_in, 16)
            sp.dma_start(xp_sb[:, :, :], xp_w.rearrange("(g p) n -> p g n", p=P)).then_inc(weights_in, 16)
            sp.dma_start(out_sb[:, :, :], out_w.rearrange("(g p) n -> p g n", p=P)).then_inc(weights_in, 16)
            sp.dma_start(rw_sb[:, :, :], router_w.rearrange("(k p) n -> p k n", p=P)).then_inc(weights_in, 16)
            load_expert(0, 0)

            for first, last, front, scan, back in PHASES:
                with sp.Fori(first, last) as i:
                    t, c, p = i, i - LEAD, i - 2 * LEAD
                    if scan:
                        sp.wait_ge(b_stored, 16 * QT * (c // QT + 1) + 16)
                        apart(sp)
                        sp.wait_ge(u_ready, STEPS * c)
                        sp.dma_start(b_bc[:, c % 2, :, :].rearrange("p n t -> p (n t)"),
                                     b_rows.rearrange("s n t -> (s n t)").rearrange("(c r) -> c r", r=NB * SEC)[c, :]
                                     .partition_broadcast(P)).then_inc(b_loaded, 16)
                    if front:
                        if back:
                            sp.wait_ge(r_done, past(p))
                        sp.wait_ge(x_loaded, 16 * (t + 1))
                        sp.dma_start(x_ring[:, (t + 1) % XR, :],
                                     x.rearrange("(t p) d -> t p d", p=P)[(t + 1) % NT, :, :])\
                            .then_inc(x_loaded, 16)
                    if back:
                        sp.wait_ge(x1_done, past(p + 1))
                        sp.dma_start(y_rows.rearrange("(t p) d -> t p d", p=P)[p, :, :],
                                     rows[:, 0, 0:DIM]).then_inc(y_stored, 16)
                    if front:
                        sp.wait_ge(xp_done, past(3 * (t + 1)))
                        sp.dma_start(b_rows[t // QT, :, tcol(t)], bt_tile[1:1 + NST, :]).then_inc(b_stored, 16)

            sp.wait_ge(scattered, 32 * NT + 16)
            sp.wait_ge(y_stored, 16 * NT + 16)
            for k in range(2):
                sp.dma_start(xg[:, k], slot_rows.rearrange("(e t p) c -> e p t c", p=P, t=ST)[k])\
                    .then_inc(xg_in[k], 16)
            load_expert(1, 1)
            with sp.Fori(1, EXPERTS // 2) as pair:
                e = 2 * pair
                for k in range(2):
                    sp.wait_ge(down_psum, past(ST * (e + k - 1)))
                    load_expert(e + k, k)
                    sp.wait_ge(eow_done, past(ST * (e + k - 1)))
                    sp.dma_start(xg[:, k], slot_rows.rearrange("(e t p) c -> e p t c", p=P, t=ST)[e + k])\
                        .then_inc(xg_in[k], 16)

            y_v = y_rows.rearrange("(s t p) d -> s p t d", p=P, t=FT)
            out_v = out.rearrange("(s t p) d -> s p t d", p=P, t=FT)
            sp.wait_ge(added, 16 * ST * EXPERTS + 16)
            for k in range(2):
                sp.dma_start(yt[:, k], y_v[k]).then_inc(yt_in[k], 16)
            for s in range(NT // FT):
                sp.wait_ge(fo_done, FT * (s + 1))
                sp.dma_start(out_v[s], yo[:, s % 2]).then_inc(out_st[s % 2], 16)
                if s + 2 < NT // FT:
                    sp.dma_start(yt[:, s % 2], y_v[s + 2]).then_inc(yt_in[s % 2], 16)
            sp.wait_ge(out_st[0], 16 * (NT // FT // 2))
            sp.wait_ge(out_st[1], 16 * (NT // FT // 2))

        @block.gpsimd
        def _(pool):
            pool.memset(ident[:, :], 0.0).then_inc(masks_made, 1)
            pool.memset(upper[:, :], 1.0).then_inc(masks_made, 1)
            pool.memset(ones[:, :], 1.0).then_inc(masks_made, 1)
            pool.iota(iota8[:, :], pattern=[[1, EXPERTS]], base=0, channel_multiplier=0,
                      allow_small_or_imprecise_dtypes=True).then_inc(masks_made, 1)
            pool.iota(token_no[:, :], pattern=[[P, NT]], base=0, channel_multiplier=1,
                      allow_small_or_imprecise_dtypes=True).then_inc(masks_made, 1)
            pool.wait_ge(masks_made, 5)
            pool.affine_select(out=ident[:, :], in_=ident[:, :], compare_op=ALU.not_equal, fill=1.0, base=0,
                               pattern=[[-1, P]], channel_multiplier=1).then_inc(masks_made, 1)
            pool.affine_select(out=upper[:, :], in_=upper[:, :], compare_op=ALU.is_gt, fill=0.0, base=0,
                               pattern=[[1, P]], channel_multiplier=-1).then_inc(masks_made, 1)
            pool.memset(zero[:, :], 0.0).then_inc(state_zeroed, 1)
            pool.memset(mhalf[:, :], -0.5).then_inc(masks_made, 1)
            pool.memset(xp0[:, :], 1.0).then_inc(state_zeroed, 1)
            pool.memset(halo[:, :, :, :], 0.0).then_inc(state_zeroed, 1)
            pool.memset(carry[:, :, :, :], 0.0).then_inc(state_zeroed, 1)
            pool.memset(taken[:, :], 0.0).then_inc(state_zeroed, 1)
            pool.memset(acc[:, :, :, :], 0.0).then_inc(state_zeroed, 1)
            pool.wait_ge(masks_made, 8)
            pool.wait_ge(empty_made, 2)
            pool.dma_start(slot_rows.rearrange("(t p) c -> p t c", p=P),
                           empty_row[:, :].rearrange("p (a c) -> p a c", a=1).to_broadcast([P, SLOTS // P, ROW]))\
                .then_inc(scattered, 16)

            def front_inverse_std(t):
                pool.wait_ge(mv1_done, t + 1)
                apart(pool)
                pool.tensor_scalar(veps[:, 0:1], mv[:, 0, 1:2], EPS, None, ALU.add).then_inc(veps1_done, 1)
                pool.wait_ge(veps1_done, t + 1)
                apart(pool)
                pool.tensor_tensor(rstd[:, 0:1], veps[:, 0:1], mhalf[:, 0:1], ALU.pow).then_inc(rstd1_done, 1)

            def back_inverse_std(p):
                pool.wait_ge(mv2_done, p + 1)
                apart(pool)
                pool.tensor_scalar(veps2[:, :], mv2[:, 1:2], EPS, None, ALU.add).then_inc(veps2_done, 1)
                pool.wait_ge(veps2_done, p + 1)
                apart(pool)
                pool.tensor_tensor(rstd2[:, :], veps2[:, :], mhalf[:, 0:1], ALU.pow).then_inc(rstd2_done, 1)

            for first, last, front, scan, back in PHASES:
                with pool.Fori(first, last) as i:
                    t, c, p = i, i - LEAD, i - 2 * LEAD
                    for k in range(STEPS):
                        j, g = k // DG, k % DG
                        if scan:
                            if k == 0:
                                pool.wait_ge(dx_done, past(QT * (c // QT) + QT))
                                pool.wait_ge(b_loaded, 16 * (c + 1))
                            pool.wait_ge(scans_done, STEPS * c + k - 3 + SCAN0)
                            apart(pool)
                            pool.tensor_tensor(u[:, k % 4, :], dx[:, (c // QT) % 2, g, :], b_bc[:, c % 2, j, :],
                                               ALU.mult).then_inc(u_ready, 1)
                        if back and k == 0:
                            pool.wait_ge(acct_done, p + 1)
                            apart(pool)
                            pool.tensor_copy(acc[:, (p // QT) % 2, p % QT, :], zero[:, 0:1].to_broadcast([P, DI]))\
                                .then_inc(acc_zeroed, 1)
                        if front and k == 1:
                            front_inverse_std(t)
                        if back and k == 9:
                            back_inverse_std(p)
                    if back:
                        pool.wait_ge(scattered, 32 * p + 16)
                        apart(pool)
                        pool.tensor_copy(rows[:, :, DIM + 1], token_no[:, bass.ds(p, 1)].to_broadcast([P, 2]))\
                            .then_inc(ids_done, 1)
                    if front:
                        pool.wait_ge(sprelu_done, past(t + 1))
                        pool.wait_ge(spln_done, t + 1)
                        if scan:
                            pool.wait_ge(scans_done, STEPS * QT * (c // QT) + SCAN0)
                        apart(pool)
                        pool.tensor_tensor(delta[:, (t // QT) % 2, :, tcol(t)], sp_ln[:, :, :], sp_relu[:, :, :],
                                           ALU.add).then_inc(delta_done, 1)
                        pool.wait_ge(delta_done, past(t + 1))
                        apart(pool)
                        pool.tensor_tensor(dx[:, (t // QT) % 2, :, tcol(t)], delta[:, (t // QT) % 2, :, tcol(t)],
                                           xc_tile[:, :, :], ALU.mult).then_inc(dx_done, 1)
                    if back:
                        pool.wait_ge(slot_done, p + 1)
                        pool.wait_ge(gate_done, past(p + 1))
                        pool.wait_ge(x1_copied, past(p + 1))
                        pool.wait_ge(ids_done, p + 1)
                        apart(pool)
                        for k in range(2):
                            pool.indirect_dma_start(
                                slot_rows[:, :], bass.IndirectOffsetOnAxis(ap=slot[:, k:k + 1], axis=0),
                                rows[:, k, :], None, bounds_check=SLOTS - 1, oob_is_err=False)\
                                .then_inc(scattered, 16)

            pool.wait_ge(scattered, 32 * NT + 16)
            pool.wait_ge(y_stored, 16 * NT + 16)
            pool.dma_start(b2_bc[:, :, :].rearrange("p e d -> p (e d)"),
                           b2.rearrange("e d -> (e d)").partition_broadcast(P)).then_inc(added, 16)

            def add_rows(e, k):
                pool.wait_ge(added, 16 * ST * e + 16)
                pool.sem_inc(landed, 1)
                apart(pool)
                pool.wait_ge(gidx_done, e + 1)
                for t in range(ST):
                    pool.wait_ge(eow_done, past(ST * e + t + 1))
                    apart(pool)
                    pool.indirect_dma_start(
                        y_rows[:, :], bass.IndirectOffsetOnAxis(ap=gidx[:, k, t:t + 1], axis=0), eo_w[:, k, t, :],
                        None, bounds_check=TOK - 1, oob_is_err=False, compute_op=ALU.add).then_inc(added, 16)

            with pool.Fori(0, EXPERTS // 2) as pair:
                e = 2 * pair
                for k in range(2):
                    add_rows(e + k, k)

            for s in range(NT // FT):
                pool.wait_ge(fmv_done, FT * (s + 1))
                pool.tensor_scalar(veps[:, :], mv[:, :, 1], EPS, None, ALU.add).then_inc(fveps_done, 1)
                pool.wait_ge(fveps_done, s + 1)
                if s:
                    pool.wait_ge(fnmr_done, s)
                pool.tensor_tensor(rstd[:, :], veps[:, :], mhalf[:, :], ALU.pow).then_inc(frstd_done, 1)

        @block.scalar
        def _(act):
            for count, credit in ((scans_done, SCAN0), (u_ready, U0), (hT_psum, HT0), (acc_done, ACC0),
                                  (carry_saved, CARRY0), (acc_zeroed, ACCZ0), (gelu_done, GEL0), (eob_done, EOB0),
                                  (b_stored, 16), (y_stored, 16)):
                act.sem_inc(count, credit)
            for count in (yT_psum, z_psum, conv_psum, xi_done, dx_done, dt_psum, delta_done, gate_done, down_psum, xp_done, pos_done, lg_done, sprelu_done, xgT_done, xnT_psum, o_psum, x1_done, x1_copied, gexp_done, cnt_psum, taken_done, eow_done, landed, r_done):
                act.sem_inc(count, 1)
            act.wait_ge(small_in, 16 * 10)
            act.activation(aexp[:, :, :], alog_sb[:, :, :], ACT.Exp).then_inc(aexp_done, 1)
            act.wait_ge(aexp_done, 1)
            act.activation(nega[:, :, :].rearrange("p n g -> p g n"), aexp[:, :, :], ACT.Copy, scale=-1.0)\
                .then_inc(nega_done, 1)
            act.wait_ge(nega_done, 1)
            act.wait_ge(state_zeroed, 6)

            def decay(c, k):
                j, g = k // DG, k % DG
                if k == 0:
                    act.wait_ge(delta_done, past(QT * (c // QT) + QT))
                act.wait_ge(scans_done, STEPS * c + k - 1 + SCAN0)
                act.activation(decay_ps[k % 2], delta[:, (c // QT) % 2, g, :], ACT.Exp,
                               scale=nega[:, bass.ds((c % QT) * NB + j, 1), g]).then_inc(decay_ready, 1)

            def take_acc(p):
                act.wait_ge(acc_done, QT * NST * (p // QT) + QT * NST + ACC0)
                act.wait_ge(yT_psum, past(p))
                act.activation(acc_tile[:, :], acc[:, (p // QT) % 2, p % QT, :], ACT.Copy)\
                    .then_inc(acct_done, 1)

            def take_xnT(t):
                act.wait_ge(xnT_psum, past(t + 1))
                act.wait_ge(z_psum, past(t))
                for k in range(KD):
                    act.activation(xnT[:, k, :], front_a[:, k * P:(k + 1) * P], ACT.Identity,
                                   bias=nb_sb[:, k:k + 1], scale=nw_sb[:, k:k + 1]).then_inc(xnT_done, 1)

            def take_xi(t):
                act.wait_ge(xi_psum, t + 1)
                act.wait_ge(conv_psum, past(t))
                act.wait_ge(xi_done, past(2 * t))
                act.activation(xi[:, :, 0:TAPS - 1], halo[:, t // TPB, :, :], ACT.Copy).then_inc(halo_in, 1)
                ps = front_b.rearrange("p (g t) -> p g t", g=DG)
                act.activation(xi[:, :, TAPS - 1:], ps, ACT.Copy).then_inc(xi_done, 1)
                act.wait_ge(halo_in, t + 1)
                apart(act)
                act.activation(halo[:, t // TPB, :, :], ps[:, :, P - TAPS + 1:P], ACT.Copy).then_inc(xi_done, 1)

            def take_z_xc(t, back, p):
                act.wait_ge(z_psum, past(t + 1))
                if back:
                    act.wait_ge(y_done, p + 1)
                    act.wait_ge(yT_psum, past(p + 1))
                act.activation(sz[:, (t // QT) % 2, :, tcol(t)], front_a.rearrange("p (g t) -> p g t", g=DG),
                               ACT.Silu).then_inc(sz_done, 1)
                act.wait_ge(conv_psum, past(t + 1))
                act.wait_ge(dx_done, past(t))
                for g in range(DG):
                    act.activation(xc_tile[:, g, :], front_b[:, g * P:(g + 1) * P], ACT.Silu,
                                   bias=cb_sb[:, g:g + 1]).then_inc(xct_done, 1)
                act.wait_ge(xct_done, DG * (t + 1))
                act.activation(xc[:, (t // QT) % 2, :, tcol(t)], xc_tile[:, :, :], ACT.Copy)\
                    .then_inc(xc_done, 1)

            def take_xp(t):
                act.wait_ge(xp_psum, t + 1)
                act.wait_ge(b_stored, 16 * t + 16)
                act.activation(bt_tile[:, :], front_a[0:1 + NST, 0:P], ACT.Copy).then_inc(xp_done, 1)
                act.wait_ge(dt_psum, past(t))
                act.activation(xp0[0:1, :], front_a[0:1, 0:P], ACT.Copy).then_inc(xp_done, 1)
                act.activation(c_sb[:, (t // QT) % 2, t % QT, :], front_a[:, P:P + NST], ACT.Copy)\
                    .then_inc(xp_done, 1)

            def softplus_parts(t):
                act.wait_ge(dt_psum, past(t + 1))
                act.wait_ge(delta_done, past(t))
                v = front_b.rearrange("p (g t) -> p g t", g=DG)
                act.activation(sp_abs[:, :, :], v, ACT.Abs).then_inc(spabs_done, 1)
                act.activation(sp_relu[:, :, :], v, ACT.Relu).then_inc(sprelu_done, 1)
                act.wait_ge(spabs_done, t + 1)
                act.activation(sp_exp[:, :, :], sp_abs[:, :, :], ACT.Exp, scale=-1.0).then_inc(spexp_done, 1)
                act.wait_ge(spexp_done, t + 1)
                act.activation(sp_ln[:, :, :], sp_exp[:, :, :], ACT.Ln, bias=1.0).then_inc(spln_done, 1)

            def take_x1T(p):
                act.wait_ge(x1_done, past(p + 1))
                act.activation(rows[:, 1, 0:DIM], rows[:, 0, 0:DIM], ACT.Copy).then_inc(x1_copied, 1)
                act.wait_ge(x1T_psum, p + 1)
                act.activation(x1T[:, :, :].rearrange("p k t -> p (k t)"), back_a[:, 0:KD * P], ACT.Copy)\
                    .then_inc(x1T_done, 1)

            def gate_exps(p):
                act.wait_ge(negmax_done, p + 1)
                act.wait_ge(gate_done, past(p))
                act.activation(gexp[:, :], logits[:, :], ACT.Exp, bias=negmax[:, 0:1], accum_out=gden[:, 0:1])\
                    .then_inc(gexp_done, 1)
                act.activation(gtop[:, :], top8[:, 0:2], ACT.Exp, bias=negmax[:, 0:1]).then_inc(gexp_done, 1)

            for first, last, front, scan, back in PHASES:
                with act.Fori(first, last) as i:
                    t, c, p = i, i - LEAD, i - 2 * LEAD
                    if back:
                        take_acc(p)
                    for k in range(STEPS):
                        if scan:
                            decay(c, k)
                        if front and k == 6:
                            take_xnT(t)
                        if front and k == 8:
                            take_xi(t)
                        if front and k == 12:
                            take_z_xc(t, back, p)
                        if back and k == 13:
                            take_x1T(p)
                        if front and k == 15:
                            if scan:
                                act.wait_ge(acc_done, QT * NST * (c // QT) + ACC0)
                            take_xp(t)
                    if front:
                        softplus_parts(t)
                    if back:
                        gate_exps(p)

            def gelu(e, k):
                act.wait_ge(down_psum, past(ST * e))
                for m in range(HG):
                    act.wait_ge(up_psum, HG * e + m + 1)
                    pair = banks[:, 2 * (m % 2):2 * (m % 2) + 2, 0:HALF]
                    act.activation(hid[:, m, :].rearrange("p (a b) -> p a b", a=2), pair, ACT.Gelu,
                                   bias=b1_sb[:, e, m:m + 1]).then_inc(gelu_done, 1)

            act.wait_ge(scattered, 32 * NT + 16)
            with act.Fori(0, EXPERTS // 2) as pair:
                e = 2 * pair
                for k in range(2):
                    gelu(e + k, k)

            for s in range(NT // FT):
                act.wait_ge(fnmr_done, s + 1)
                act.wait_ge(yt_in[s % 2], 16 * (s // 2 + 1))
                if s >= 2:
                    act.wait_ge(out_st[s % 2], 16 * (s // 2))
                for n in range(FT):
                    act.activation(yo[:, s % 2, n, :], yt[:, s % 2, n, :], ACT.Identity,
                                   bias=nmr[:, s % 2, n:n + 1], scale=rstd2x[:, s % 2, n:n + 1])\
                        .then_inc(fo_done, 1)

        @block.tensor
        def _(pe):
            pe.wait_ge(weights_in, 16 * 4)
            pe.wait_ge(small_in, 16 * 10)
            pe.wait_ge(masks_made, 8)
            pe.wait_ge(consts_made, 2 + DG * TAPS + DG)
            pe.wait_ge(state_zeroed, 6)

            def state_sums(c, k):
                j, tt = k // DG, k % DG
                if tt == 0:
                    pe.wait_ge(scans_done, STEPS * c + DG * (j + 1) + SCAN0)
                pe.wait_ge(acc_done, STEPS * c + k - 1 + ACC0)
                for g in range(DG):
                    mm = pe.transpose(hT_ps[k % 2][:, g * P:(g + 1) * P], h[:, j % 2, g, tt * P:(tt + 1) * P],
                                      ident[:, :])
                mm.then_inc(hT_psum, 1)

            def x_norm_T(t):
                pe.wait_ge(xn_done, t + 1)
                pe.wait_ge(xp_done, past(3 * t))
                for k in range(KD):
                    mm = pe.transpose(front_a[:, k * P:(k + 1) * P], xn[:, k * P:(k + 1) * P], ident[:, :])
                mm.then_inc(xnT_psum, 1)

            def project_in(half, bank, ready):
                for m in range(DG):
                    for k in range(KD):
                        mm = pe.matmul(bank[:, m * P:(m + 1) * P],
                                       in_sb[:, k, half * DI + m * P:half * DI + (m + 1) * P], xnT[:, k, :],
                                       start=(k == 0), stop=(k == KD - 1))
                mm.then_inc(ready, 1)

            def convolve(t, g0, g1):
                for g in range(g0, g1):
                    for j in range(TAPS):
                        mm = pe.matmul(front_b[:, g * P:(g + 1) * P], conv_diag[:, g, j, :], xi[:, g, j:j + P],
                                       start=(j == 0), stop=(j == TAPS - 1))
                if g1 == DG:
                    mm.then_inc(conv_psum, 1)

            def project_x(t):
                pe.wait_ge(sz_done, t + 1)
                pe.wait_ge(xct_done, DG * (t + 1))
                for g in range(DG):
                    pe.matmul(front_a[0:1 + NST, 0:P], xp_sb[:, g, 0:1 + NST], xc_tile[:, g, :],
                              start=(g == 0), stop=(g == DG - 1))
                for g in range(DG):
                    mm = pe.matmul(front_a[:, P:P + NST], xc_tile[:, g, :], xp_sb[:, g, 1 + NST:],
                                   start=(g == 0), stop=(g == DG - 1))
                mm.then_inc(xp_psum, 1)

            def project_dt(t):
                pe.wait_ge(xp_done, past(3 * (t + 1)))
                pe.wait_ge(xct_done, DG * (t + 1))
                for g in range(DG):
                    mm = pe.matmul(front_b[:, g * P:(g + 1) * P], dt_sb[:, g * P:(g + 1) * P], xp0[:, :],
                                   start=True, stop=True)
                mm.then_inc(dt_psum, 1)

            def y_channels(p):
                pe.wait_ge(acct_done, p + 1)
                pe.wait_ge(pos_done, past(2 * p))
                for g in range(DG):
                    pe.matmul(back_a[:, g * P:(g + 1) * P], acc_tile[:, g * P:(g + 1) * P], ident[:, :],
                              start=True, stop=False)
                    mm = pe.matmul(back_a[:, g * P:(g + 1) * P], skip_diag[:, g, :],
                                   xc[:, (p // QT) % 2, g, tcol(p)], start=False, stop=True)
                mm.then_inc(yT_psum, 1)

            def project_out(p):
                pe.wait_ge(y_done, p + 1)
                pe.wait_ge(lg_done, past(p))
                for g in range(DG):
                    mm = pe.matmul(back_b[:, 0:DIM], y_tile[:, g, :], out_sb[:, g, :],
                                   start=(g == 0), stop=(g == DG - 1))
                mm.then_inc(o_psum, 1)

            def x1_T(p):
                pe.wait_ge(x1_done, past(p + 1))
                for k in range(KD):
                    mm = pe.transpose(back_a[:, k * P:(k + 1) * P], rows[:, 0, k * P:(k + 1) * P], ident[:, :])
                mm.then_inc(x1T_psum, 1)

            def route(p):
                pe.wait_ge(x1T_done, p + 1)
                pe.wait_ge(r_done, past(p + 1))
                for k in range(KD):
                    mm = pe.matmul(back_b[:, 0:EXPERTS], x1T[:, k, :], rw_sb[:, k, :],
                                   start=(k == 0), stop=(k == KD - 1))
                mm.then_inc(lg_psum, 1)

            def count(p):
                pe.wait_ge(mask_done, p + 1)
                pe.matmul(back_a[:, 0:EXPERTS], upper_b[:, :], mask_b[:, :], start=True, stop=True)
                pe.matmul(back_a[:, EXPERTS:2 * EXPERTS], ones_b[:, :], mask_b[:, :], start=True, stop=True)\
                    .then_inc(cnt_psum, 1)

            for first, last, front, scan, back in PHASES:
                with pe.Fori(first, last) as i:
                    t, c, p = i, i - LEAD, i - 2 * LEAD
                    for k in range(STEPS):
                        if scan:
                            state_sums(c, k)
                        if back and k == 0:
                            y_channels(p)
                        if front and k == 1:
                            x_norm_T(t)
                        if front and k == 2:
                            pe.wait_ge(xnT_done, KD * (t + 1))
                            pe.wait_ge(sprelu_done, past(t))
                            project_in(0, front_b, xi_psum)
                        if back and k == 3:
                            project_out(p)
                        if front and k == 4:
                            project_in(1, front_a, z_psum)
                        if front and k == 6:
                            pe.wait_ge(xi_done, past(2 * (t + 1)))
                            convolve(t, 0, 2)
                        if front and k == 7:
                            convolve(t, 2, DG)
                        if back and k == 8:
                            x1_T(p)
                        if front and k == 9:
                            project_x(t)
                        if back and k == 10:
                            route(p)
                        if front and k == 12:
                            project_dt(t)
                        if back and k == 13:
                            count(p)

            def gathered_T(e, k, kd):
                if kd == 0:
                    pe.wait_ge(xg_in[k], 8 * (e - k) + 16)
                pe.wait_ge(xgT_done, past(KD * e + kd))
                for t in range(ST):
                    mm = pe.transpose(banks[:, 6:8, :].rearrange("p a b -> p (a b)")[:, t * P:(t + 1) * P],
                                      xg[:, k, t, kd * P:(kd + 1) * P], ident[:, :])
                mm.then_inc(xgT_psum, 1)

            def expert(e, k, following):
                pe.wait_ge(w_in[k], 16 * (e - k) + 32)
                pe.wait_ge(xgT_done, past(KD * (e + 1)))
                for m in range(HG):
                    pe.wait_ge(gelu_done, HG * e + m - 1 + GEL0)
                    for a in range(2):
                        for kd in range(KD):
                            mm = pe.matmul(banks[:, 2 * (m % 2) + a, 0:HALF], w1_sb[k][:, kd, m * P:(m + 1) * P],
                                           xgT[:, k, kd, a * HALF:(a + 1) * HALF],
                                           start=(kd == 0), stop=(kd == KD - 1))
                    mm.then_inc(up_psum, 1)
                    if following and m in (3, 7):
                        gathered_T(e + 1, 1 - k, m // 4)
                pe.wait_ge(gelu_done, HG * (e + 1) + GEL0)
                for t in range(ST):
                    pe.wait_ge(eob_done, ST * e + t - 1 + EOB0)
                    for m in range(HG):
                        mm = pe.matmul(banks[:, 4 + (ST * k + t) % 2, 0:DIM], hid[:, m, t * P:(t + 1) * P],
                                       w2_sb[k][:, m, :], start=(m == 0), stop=(m == HG - 1))
                    mm.then_inc(down_psum, 1)

            pe.wait_ge(scattered, 32 * NT + 16)
            gathered_T(0, 0, 0)
            gathered_T(0, 0, 1)
            with pe.Fori(0, EXPERTS // 2 - 1) as pair:
                e = 2 * pair
                expert(e, 0, True)
                expert(e + 1, 1, True)
            expert(EXPERTS - 2, 0, True)
            expert(EXPERTS - 1, 1, False)

        @block.vector
        def _(dve):
            dve.memset(empty_row[:, 0:ROW - 1], 0.0).then_inc(empty_made, 1)
            dve.memset(empty_row[:, ROW - 1:ROW], FAR).then_inc(empty_made, 1)
            dve.wait_ge(masks_made, 8)
            dve.wait_ge(small_in, 16 * 10)
            dve.tensor_copy(ones_b[:, :], ones[:, :]).then_inc(consts_made, 1)
            dve.tensor_copy(upper_b[:, :], upper[:, :]).then_inc(consts_made, 1)
            for g in range(DG):
                for j in range(TAPS):
                    dve.tensor_scalar(conv_diag[:, g, j, :], ident[:, :], cw_sb[:, g, j:j + 1], None, ALU.mult)\
                        .then_inc(consts_made, 1)
            for g in range(DG):
                dve.tensor_scalar(skip_diag[:, g, :], ident[:, :], ds_sb[:, g:g + 1], None, ALU.mult)\
                    .then_inc(consts_made, 1)
            dve.wait_ge(state_zeroed, 6)

            def scan_step(c, k):
                j, g = k // DG, k % DG
                if g == 0:
                    dve.wait_ge(hT_psum, DG * (NB * c + j) - 4 + HT0)
                    dve.wait_ge(carry_saved, NB * c + j - 1 + CARRY0)
                dve.wait_ge(u_ready, STEPS * c + k + 1 + U0)
                dve.wait_ge(decay_ready, STEPS * c + k + 1)
                dve.tensor_tensor_scan(h[:, j % 2, g, :], decay_ps[k % 2], u[:, k % 4, :],
                                       carry[:, c // TPB, bass.ds((c % QT) * NB + j, 1), g],
                                       ALU.mult, ALU.add).then_inc(scans_done, 1)

            def save_carry(c, j):
                dve.wait_ge(scans_done, STEPS * c + DG * (j + 1) + SCAN0)
                apart(dve)
                dve.tensor_copy(carry[:, c // TPB, bass.ds((c % QT) * NB + j, 1), :]
                                .rearrange("p a g -> p (a g)"), h[:, j % 2, :, SEC - 1])\
                    .then_inc(carry_saved, 1)

            def add_state(c, j, tt):
                n = STEPS * c + DG * j + tt
                if j == 0 and tt == 0:
                    dve.wait_ge(acc_zeroed, QT * (c // QT) - QT + ACCZ0)
                    dve.wait_ge(xp_done, past(3 * QT * (c // QT) + 3 * QT))
                dve.wait_ge(hT_psum, n + 1 + HT0)
                dve.wait_ge(acc_done, n - 3 + ACC0)
                a = acc[:, (c // QT) % 2, tt, :]
                dve.scalar_tensor_tensor(out=a, in0=hT_ps[tt % 2],
                                         scalar=c_sb[:, (c // QT) % 2, tt, bass.ds((c % QT) * NB + j, 1)],
                                         in1=a, op0=ALU.mult, op1=ALU.add).then_inc(acc_done, 1)

            def front_stats(t):
                dve.wait_ge(x_loaded, 16 * (t + 1))
                dve.bn_stats(stat[:, 0, :], x_ring[:, t % XR, :]).then_inc(st1_done, 1)
                dve.wait_ge(st1_done, t + 1)
                apart(dve)
                dve.bn_aggr(mv[:, 0, :], stat[:, 0, :]).then_inc(mv1_done, 1)

            def front_norm(t):
                dve.wait_ge(rstd1_done, t + 1)
                dve.wait_ge(xnT_psum, past(t))
                dve.tensor_scalar(xn[:, :], x_ring[:, t % XR, :], mv[:, 0, 0:1], rstd[:, 0:1],
                                  ALU.subtract, ALU.mult).then_inc(xn_done, 1)

            def gate_y(p):
                dve.wait_ge(yT_psum, past(p + 1))
                dve.wait_ge(o_psum, past(p))
                dve.tensor_tensor(y_tile[:, :, :], back_a.rearrange("p (g t) -> p g t", g=DG),
                                  sz[:, (p // QT) % 2, :, tcol(p)], ALU.mult).then_inc(y_done, 1)

            def residual(p):
                dve.wait_ge(o_psum, past(p + 1))
                dve.wait_ge(x1_done, past(p))
                dve.scalar_tensor_tensor(out=r_tile[:, :], in0=x_ring[:, p % XR, :], scalar=2.0,
                                         in1=back_b[:, 0:DIM], op0=ALU.mult, op1=ALU.add)\
                    .then_inc(r_done, 1)
                dve.wait_ge(r_done, past(p + 1))
                dve.bn_stats(stat2[:, :], r_tile[:, :]).then_inc(st2_done, 1)
                dve.wait_ge(st2_done, p + 1)
                apart(dve)
                dve.bn_aggr(mv2[:, :], stat2[:, :]).then_inc(mv2_done, 1)

            def norm_x1(p):
                dve.wait_ge(rstd2_done, p + 1)
                dve.wait_ge(y_stored, 16 * p + 16)
                dve.wait_ge(scattered, 32 * p + 16)
                dve.wait_ge(x1_copied, past(p))
                dve.tensor_scalar(rows[:, 0, 0:DIM], r_tile[:, :], mv2[:, 0:1], rstd2[:, 0:1],
                                  ALU.subtract, ALU.mult).then_inc(x1_done, 1)

            def choose(p):
                dve.wait_ge(lg_psum, p + 1)
                dve.wait_ge(gexp_done, past(2 * p))
                dve.tensor_tensor(logits[:, :], back_b[:, 0:EXPERTS], rb_sb[:, :], ALU.add)\
                    .then_inc(lg_done, 1)
                dve.wait_ge(lg_done, past(p + 1))
                apart(dve)
                dve.max(top8[:, :], logits[:, :]).then_inc(top_done, 1)
                dve.wait_ge(top_done, p + 1)
                apart(dve)
                dve.max_index(idx8[:, :], top8[:, :], logits[:, :]).then_inc(idx_done, 1)
                dve.tensor_scalar(negmax[:, :], top8[:, 0:1], -1.0, None, ALU.mult).then_inc(negmax_done, 1)
                dve.wait_ge(idx_done, p + 1)
                dve.tensor_copy(idxf[:, :], idx8[:, 0:2]).then_inc(idxf_done, 1)
                dve.wait_ge(idxf_done, p + 1)
                for k in range(2):
                    dve.tensor_scalar(choice[:, k, :], iota8[:, :], idxf[:, k:k + 1], None, ALU.is_equal)\
                        .then_inc(choice_done, 1)
                dve.wait_ge(choice_done, 2 * (p + 1))
                dve.wait_ge(cnt_psum, past(p))
                dve.tensor_tensor(mask_b[:, :], choice[:, 0, :], choice[:, 1, :], ALU.add)\
                    .then_inc(mask_done, 1)

            def place(p):
                dve.wait_ge(cnt_psum, past(p + 1))
                dve.wait_ge(taken_done, past(p))
                dve.tensor_tensor(pos[:, :], back_a[:, 0:EXPERTS], taken[:, :], ALU.add)\
                    .then_inc(pos_done, 1)
                dve.wait_ge(pos_done, past(2 * p + 1))
                dve.tensor_tensor(taken[:, :], back_a[:, EXPERTS:2 * EXPERTS], taken[:, :], ALU.add)\
                    .then_inc(pos_done, 1)
                dve.wait_ge(pos_done, past(2 * p + 2))
                dve.tensor_tensor(pick[:, :, :], choice[:, :, :],
                                  pos[:, :].rearrange("p (a e) -> p a e", a=1).to_broadcast([P, 2, EXPERTS]),
                                  ALU.mult).then_inc(taken_done, 1)
                dve.wait_ge(taken_done, past(p + 1))
                dve.tensor_reduce(posk[:, :], pick[:, :, :], mybir.AxisListType.X, ALU.add)\
                    .then_inc(pick_done, 1)
                dve.wait_ge(gexp_done, past(2 * (p + 1)))
                dve.reciprocal(grec[:, :], gden[:, :]).then_inc(grec_done, 1)
                dve.wait_ge(pick_done, p + 1)
                dve.scalar_tensor_tensor(out=slotf[:, :], in0=idxf[:, :], scalar=float(CAP), in1=posk[:, :],
                                         op0=ALU.mult, op1=ALU.add).then_inc(slotf_done, 1)
                dve.tensor_scalar(over[:, :], posk[:, :], float(CAP), FAR, ALU.is_ge, ALU.mult)\
                    .then_inc(over_done, 1)
                dve.wait_ge(grec_done, p + 1)
                dve.tensor_scalar(rows[:, :, DIM], gtop[:, :], grec[:, 0:1], None, ALU.mult)\
                    .then_inc(gate_done, 1)
                dve.wait_ge(slotf_done, p + 1)
                dve.wait_ge(over_done, p + 1)
                dve.tensor_tensor(slot[:, :], slotf[:, :], over[:, :], ALU.add).then_inc(slot_done, 1)

            for first, last, front, scan, back in PHASES:
                with dve.Fori(first, last) as i:
                    t, c, p = i, i - LEAD, i - 2 * LEAD
                    for k in range(STEPS):
                        j, g = k // DG, k % DG
                        if scan:
                            scan_step(c, k)
                            if j >= 1:
                                add_state(c, j - 1, g)
                                if g == 0:
                                    save_carry(c, j - 1)
                        if front and k == 0:
                            front_stats(t)
                        if front and k == 2:
                            front_norm(t)
                        if back and k == 5:
                            gate_y(p)
                        if back and k == 9:
                            residual(p)
                        if back and k == 11:
                            norm_x1(p)
                    if back:
                        choose(p)
                    if scan:
                        save_carry(c, NB - 1)
                        for tt in range(QT):
                            add_state(c, NB - 1, tt)
                    if back:
                        place(p)

            def take_gathered(e, k):
                dve.wait_ge(xg_in[k], 8 * (e - k) + 16)
                dve.wait_ge(landed, past(e))
                dve.tensor_copy(gidx[:, k, :], xg[:, k, :, ROW - 1]).then_inc(gidx_done, 1)
                for kd in range(KD):
                    dve.wait_ge(xgT_psum, KD * e + kd + 1)
                    dve.tensor_copy(xgT[:, k, kd, :],
                                    banks[:, 6:8, :].rearrange("p a b -> p (a b)")[:, 0:CAP])\
                        .then_inc(xgT_done, 1)

            def weigh(e, k, following):
                if following:
                    take_gathered(e + 1, 1 - k)
                dve.wait_ge(landed, past(e))
                dve.wait_ge(eow_done, past(ST * e))
                for t in range(ST):
                    dve.wait_ge(down_psum, past(ST * e + t + 1))
                    dve.tensor_tensor(eo[:, t, :], banks[:, 4 + (ST * k + t) % 2, 0:DIM], b2_bc[:, e, :],
                                      ALU.add).then_inc(eob_done, 1)
                    dve.wait_ge(eob_done, ST * e + t + 1 + EOB0)
                    dve.tensor_scalar(eo_w[:, k, t, :], eo[:, t, :], xg[:, k, t, DIM:DIM + 1], None, ALU.mult)\
                        .then_inc(eow_done, 1)

            dve.wait_ge(added, 16)
            take_gathered(0, 0)
            with dve.Fori(0, EXPERTS // 2 - 1) as pair:
                e = 2 * pair
                weigh(e, 0, True)
                weigh(e + 1, 1, True)
            weigh(EXPERTS - 2, 0, True)
            weigh(EXPERTS - 1, 1, False)

            for s in range(NT // FT):
                dve.wait_ge(yt_in[s % 2], 16 * (s // 2 + 1))
                if s:
                    dve.wait_ge(fnmr_done, s)
                for n in range(FT):
                    dve.bn_stats(stat[:, n, :], yt[:, s % 2, n, :]).then_inc(fst_done, 1)
                for n in range(FT):
                    dve.wait_ge(fst_done, FT * s + n + 1)
                    dve.bn_aggr(mv[:, n, :], stat[:, n, :]).then_inc(fmv_done, 1)
                dve.wait_ge(frstd_done, s + 1)
                if s >= 2:
                    dve.wait_ge(fo_done, FT * (s - 1))
                dve.tensor_copy(rstd2x[:, s % 2, :], rstd[:, :]).then_inc(fr_copied, 1)
                dve.wait_ge(fr_copied, s + 1)
                dve.scalar_tensor_tensor(out=nmr[:, s % 2, :], in0=mv[:, :, 0], scalar=-1.0, in1=rstd[:, :],
                                         op0=ALU.mult, op1=ALU.mult).then_inc(fnmr_done, 1)


_INS = ["x", "norm_w", "norm_b", "in_proj_w", "conv_w", "conv_b", "x_proj_w", "dt_w", "dt_b", "A_log", "D_skip",
        "out_proj_w", "router_w", "router_b", "w1", "b1", "w2", "b2"]


def kernel(**inputs):
    import numpy as _np
    import concourse.bacc as _bacc
    from concourse import mybir as _mybir
    from concourse.bass_utils import run_bass_kernel_spmd as _run

    nc = _bacc.Bacc("TRN2", target_bir_lowering=False, num_devices=1)
    arrays, args = {}, []
    for name in _INS:
        part = "L0_ffn_" if name in ("router_w", "router_b", "w1", "b1", "w2", "b2") else "L0_attn_"
        a = _np.asarray(inputs[part + name])
        if name == "x":
            a = a.reshape(-1, a.shape[-1])
        if name in ("in_proj_w", "x_proj_w", "out_proj_w"):
            a = a.T
        if name in ("norm_w", "norm_b", "conv_b", "D_skip"):
            a = a.reshape(-1, P).T
        if name == "dt_w":
            a = a.T
        if name == "b1":
            a = a.reshape(EXPERTS, HG, P).transpose(2, 0, 1)
        a = _np.ascontiguousarray(a)
        arrays[f"in_{name}_dram"] = a
        args.append(nc.dram_tensor(f"in_{name}_dram", a.shape, _mybir.dt.from_np(a.dtype), kind="ExternalInput").ap())
    out = nc.dram_tensor("out_0_dram", (TOK, DIM), F32, kind="ExternalOutput").ap()
    build(nc, *args, out)
    r = _run(nc, [arrays], core_ids=[0])
    return r.results[0]["out_0_dram"].reshape(BATCH, SEQ, DIM)
```

```python
from contextlib import ExitStack

import concourse.bass as bass
from concourse import mybir

F32 = mybir.dt.float32
BF16 = mybir.dt.bfloat16
U32 = mybir.dt.uint32
ALU = mybir.AluOpType
ACT = mybir.ActivationFunctionType

P = 128
DIM = 256
DI = 512
DG = DI // P
KD = DIM // P
NST = 16
TAPS = 4
BATCH, SEQ = 2, 2048
TOK = BATCH * SEQ
NT = TOK // P
SEC = 512
QT = SEC // P
NB = NST // QT
STEPS = NB * DG
TPB = SEQ // P
XR = 12
EXPERTS, HID, CAP = 8, 1024, 640
SLOTS = EXPERTS * CAP
ST = CAP // P
HG = HID // P
HALF = CAP // 2
ROW = DIM + 2
EPS = 1e-5
FAR = 1.0e6
LEAD = QT + 1
BACK = LEAD + QT
RT = 9
LAG = 5
FT = 4

SCAN0 = STEPS
U0 = 2 * STEPS
HT0 = 4
ACC0 = 4
CARRY0 = NST
ACCZ0 = QT
GEL0 = 2
EOB0 = 2


def past(n):
    return n + 1


def build(nc, x, norm_w, norm_b, in_w, conv_w, conv_b, xp_w, dt_w, dt_b, a_log, d_skip, out_w,
          router_w, router_b, w1, b1, w2, b2, out):
    with ExitStack() as ctx:
        scope = [ctx]

        def sb(name, shape, dt=F32):
            return scope[0].enter_context(nc.sbuf_tensor(name, shape, dt))

        def sem(name):
            return ctx.enter_context(nc.semaphore(name))

        b_rows = nc.dram_tensor("b_rows", [NT // QT, NST, SEC], F32, kind="Internal").ap()
        slot_rows = nc.dram_tensor("slot_rows", [SLOTS, ROW], F32, kind="Internal").ap()
        y_rows = nc.dram_tensor("y_rows", [TOK, DIM], F32, kind="Internal").ap()

        banks = ctx.enter_context(nc.psum_tensor("banks", [P, 8, 512], F32))
        decay_ps = [banks[:, 0, :], banks[:, 1, :]]
        hT_ps = [banks[:, 2, :], banks[:, 3, :]]
        front_a, front_b = banks[:, 4, :], banks[:, 5, :]
        back_a, back_b = banks[:, 6, :], banks[:, 7, :]

        ident = sb("ident", [P, P])
        w1_sb = [sb("w1_even", [P, KD, HID])]
        w2_sb = [sb("w2_even", [P, HG, DIM])]
        b1_sb = sb("b1_sb", [P, EXPERTS, HG])
        mhalf = sb("mhalf", [P, FT])
        stat = sb("stat", [P, FT, 6])
        mv = sb("mv", [P, FT, 2])
        veps = sb("veps", [P, FT])
        rstd = sb("rstd", [P, FT])

        ssm = ExitStack()
        scope[0] = ssm
        in_sb = sb("in_sb", [P, KD, 2 * DI])
        out_sb = sb("out_sb", [P, DG, DIM])
        xp_sb = sb("xp_sb", [P, DG, 1 + 2 * NST])
        rw_sb = sb("rw_sb", [P, KD, EXPERTS])
        rb_sb = sb("rb_sb", [P, EXPERTS])
        nw_sb = sb("nw_sb", [P, KD])
        nb_sb = sb("nb_sb", [P, KD])
        cw_sb = sb("cw_sb", [P, DG, TAPS])
        cb_sb = sb("cb_sb", [P, DG])
        ds_sb = sb("ds_sb", [P, DG])
        dt_sb = sb("dt_sb", [2, DI])
        alog_sb = sb("alog_sb", [P, DG, NST])
        aexp = sb("aexp", [P, DG, NST])
        nega = sb("nega", [P, NST, DG])
        conv_diag = sb("conv_diag", [P, DG, TAPS, P])
        skip_diag = sb("skip_diag", [P, DG, P])
        ones = sb("ones", [P, P])
        zero = sb("zero", [P, 1])
        ones_b = sb("ones_b", [P, P], BF16)
        upper = sb("upper", [P, P])
        upper_b = sb("upper_b", [P, P], BF16)
        iota8 = sb("iota8", [P, EXPERTS])
        token_no = sb("token_no", [P, NT])
        empty_row = sb("empty_row", [P, ROW])

        x_ring = sb("x_ring", [P, XR, DIM])
        xn = sb("xn", [P, DIM])
        xnT = sb("xnT", [P, KD, P])
        xi = sb("xi", [P, DG, TAPS - 1 + P])
        halo = sb("halo", [P, BATCH, DG, TAPS - 1])
        xc_tile = sb("xc_tile", [P, DG, P])
        xc = sb("xc", [P, RT, DG, P])
        sz = sb("sz", [P, RT, DG, P])
        bt_tile = sb("bt_tile", [1 + NST, P])
        xp0 = sb("xp0", [2, P])
        c_sb = sb("c_sb", [P, 2, QT, NST])
        sp_abs = sb("sp_abs", [P, DG, P])
        sp_exp = sb("sp_exp", [P, DG, P])
        sp_ln = sb("sp_ln", [P, DG, P])
        sp_relu = sb("sp_relu", [P, DG, P])
        delta = sb("delta", [P, 2, DG, SEC])
        dx = sb("dx", [P, 2, DG, SEC])
        b_bc = sb("b_bc", [P, 2, NB, SEC])
        u = sb("u", [P, 4, SEC])
        h = sb("h", [P, 2, DG, SEC])
        carry = sb("carry", [P, BATCH, NST, DG])
        acc = sb("acc", [P, 2, QT, DI])
        acc_tile = sb("acc_tile", [P, DI])
        y_tile = sb("y_tile", [P, DG, P])
        r_tile = sb("r_tile", [P, DIM])
        stat2 = sb("stat2", [P, 6])
        mv2 = sb("mv2", [P, 2])
        veps2 = sb("veps2", [P, 1])
        rstd2 = sb("rstd2", [P, 1])
        rows = sb("rows", [P, 2, ROW])
        x1T = sb("x1T", [P, KD, P])
        logits = sb("logits", [P, EXPERTS])
        top8 = sb("top8", [P, 8])
        idx8 = sb("idx8", [P, 8], U32)
        idxf = sb("idxf", [P, 2])
        choice = sb("choice", [P, 2, EXPERTS])
        mask_b = sb("mask_b", [P, EXPERTS], BF16)
        negmax = sb("negmax", [P, 1])
        gexp = sb("gexp", [P, EXPERTS])
        gden = sb("gden", [P, 1])
        gtop = sb("gtop", [P, 2])
        grec = sb("grec", [P, 1])
        taken = sb("taken", [P, EXPERTS])
        pos = sb("pos", [P, EXPERTS])
        pick = sb("pick", [P, 2, EXPERTS])
        posk = sb("posk", [P, 2])
        slotf = sb("slotf", [P, 2])
        over = sb("over", [P, 2])
        slot = sb("slot", [P, 2], U32)
        ssm.close()

        ffn = ExitStack()
        ctx.enter_context(ffn)
        scope[0] = ffn
        w1_sb.append(sb("w1_odd", [P, KD, HID]))
        w2_sb.append(sb("w2_odd", [P, HG, DIM]))
        xg = sb("xg", [P, 2, ST, ROW])
        gidx = sb("gidx", [P, 2, ST], U32)
        xgT = sb("xgT", [P, 2, KD, CAP])
        hid = sb("hid", [P, HG, CAP])
        b2_bc = sb("b2_bc", [P, EXPERTS, DIM])
        eo = sb("eo", [P, ST, DIM])
        eo_w = sb("eo_w", [P, 2, ST, DIM])
        yt = sb("yt", [P, 2, FT, DIM])
        yo = sb("yo", [P, 2, FT, DIM])
        rstd2x = sb("rstd2x", [P, 2, FT])
        nmr = sb("nmr", [P, 2, FT])

        weights_in = sem("weights_in")
        small_in = sem("small_in")
        x_loaded = sem("x_loaded")
        masks_made = sem("masks_made")
        consts_made = sem("consts_made")
        empty_made = sem("empty_made")
        state_zeroed = sem("state_zeroed")
        aexp_done = sem("aexp_done")
        nega_done = sem("nega_done")
        st1_done = sem("st1_done")
        mv1_done = sem("mv1_done")
        veps1_done = sem("veps1_done")
        rstd1_done = sem("rstd1_done")
        xn_done = sem("xn_done")
        xnT_psum = sem("xnT_psum")
        xnT_done = sem("xnT_done")
        xi_psum = sem("xi_psum")
        z_psum = sem("z_psum")
        halo_in = sem("halo_in")
        xi_done = sem("xi_done")
        conv_psum = sem("conv_psum")
        sz_done = sem("sz_done")
        xct_done = sem("xct_done")
        xc_done = sem("xc_done")
        xp_psum = sem("xp_psum")
        xp_done = sem("xp_done")
        b_stored = sem("b_stored")
        b_loaded = sem("b_loaded")
        dt_psum = sem("dt_psum")
        spabs_done = sem("spabs_done")
        spexp_done = sem("spexp_done")
        spln_done = sem("spln_done")
        sprelu_done = sem("sprelu_done")
        delta_done = sem("delta_done")
        dx_done = sem("dx_done")
        u_ready = sem("u_ready")
        decay_ready = sem("decay_ready")
        scans_done = sem("scans_done")
        carry_saved = sem("carry_saved")
        hT_psum = sem("hT_psum")
        acc_done = sem("acc_done")
        acct_done = sem("acct_done")
        acc_zeroed = sem("acc_zeroed")
        yT_psum = sem("yT_psum")
        y_done = sem("y_done")
        o_psum = sem("o_psum")
        r_done = sem("r_done")
        st2_done = sem("st2_done")
        mv2_done = sem("mv2_done")
        veps2_done = sem("veps2_done")
        rstd2_done = sem("rstd2_done")
        x1_done = sem("x1_done")
        x1_copied = sem("x1_copied")
        y_stored = sem("y_stored")
        ids_done = sem("ids_done")
        x1T_psum = sem("x1T_psum")
        x1T_done = sem("x1T_done")
        lg_psum = sem("lg_psum")
        lg_done = sem("lg_done")
        top_done = sem("top_done")
        idx_done = sem("idx_done")
        idxf_done = sem("idxf_done")
        choice_done = sem("choice_done")
        mask_done = sem("mask_done")
        negmax_done = sem("negmax_done")
        gexp_done = sem("gexp_done")
        grec_done = sem("grec_done")
        gate_done = sem("gate_done")
        cnt_psum = sem("cnt_psum")
        pos_done = sem("pos_done")
        taken_done = sem("taken_done")
        pick_done = sem("pick_done")
        slotf_done = sem("slotf_done")
        over_done = sem("over_done")
        slot_done = sem("slot_done")
        scattered = sem("scattered")
        gidx_done = sem("gidx_done")
        xgT_psum = sem("xgT_psum")
        xgT_done = sem("xgT_done")
        up_psum = sem("up_psum")
        gelu_done = sem("gelu_done")
        down_psum = sem("down_psum")
        eob_done = sem("eob_done")
        eow_done = sem("eow_done")
        added = sem("added")
        landed = sem("landed")
        fst_done = sem("fst_done")
        fmv_done = sem("fmv_done")
        fveps_done = sem("fveps_done")
        frstd_done = sem("frstd_done")
        fo_done = sem("fo_done")
        fr_copied = sem("fr_copied")
        fnmr_done = sem("fnmr_done")
        w_in = [sem("w_in_even"), sem("w_in_odd")]
        xg_in = [sem("xg_in_even"), sem("xg_in_odd")]
        yt_in = [sem("yt_in_even"), sem("yt_in_odd")]
        out_st = [sem("out_st_even"), sem("out_st_odd")]

        def apart(eng):
            eng.nop(nofuse=True)

        PHASES = [(0, 1, "A"), (1, LEAD, "AB"), (LEAD, BACK, "ABC"), (BACK, NT, "ABCD"), (NT, NT + 1, "BCD"),
                  (NT + 1, NT + LEAD, "CD"), (NT + LEAD, NT + BACK, "D")]

        def tcol(t):
            return bass.ds((t % QT) * P, P)

        block = ctx.enter_context(nc.Block())

        @block.sync
        def _(sp):
            def load_expert(e, k):
                sp.dma_start(w1_sb[k][:, :, :], w1[e].rearrange("(k p) n -> p k n", p=P)).then_inc(w_in[k], 16)
                sp.dma_start(w2_sb[k][:, :, :], w2[e].rearrange("(g p) n -> p g n", p=P)).then_inc(w_in[k], 16)

            sp.dma_start(in_sb[:, :, :], in_w.rearrange("(k p) n -> p k n", p=P)).then_inc(weights_in, 16)
            sp.dma_start(x_ring[:, 0, :], x[0:P, :]).then_inc(x_loaded, 16)
            for dst, src in ((nw_sb[:, :], norm_w),
                             (nb_sb[:, :], norm_b),
                             (cw_sb[:, :, :], conv_w.rearrange("(g p) o j -> p g (o j)", p=P)),
                             (cb_sb[:, :], conv_b),
                             (ds_sb[:, :], d_skip),
                             (dt_sb[0:1, :], dt_w),
                             (dt_sb[1:2, :], dt_b.rearrange("(o d) -> o d", o=1)),
                             (alog_sb[:, :, :], a_log.rearrange("(g p) n -> p g n", p=P)),
                             (b1_sb[:, :, :], b1),
                             (rb_sb[:, :], router_b.partition_broadcast(P))):
                sp.dma_start(dst, src).then_inc(small_in, 16)
            sp.dma_start(xp_sb[:, :, :], xp_w.rearrange("(g p) n -> p g n", p=P)).then_inc(weights_in, 16)
            sp.dma_start(out_sb[:, :, :], out_w.rearrange("(g p) n -> p g n", p=P)).then_inc(weights_in, 16)
            sp.dma_start(rw_sb[:, :, :], router_w.rearrange("(k p) n -> p k n", p=P)).then_inc(weights_in, 16)
            load_expert(0, 0)

            for first, last, stages in PHASES:
                with sp.Fori(first, last) as i:
                    t, c, p = i, i - LEAD, i - BACK
                    if "C" in stages:
                        sp.wait_ge(b_stored, 16 * QT * (c // QT + 1) + 16)
                        apart(sp)
                        sp.wait_ge(u_ready, STEPS * c + U0 - STEPS)
                        sp.dma_start(b_bc[:, c % 2, :, :].rearrange("p n t -> p (n t)"),
                                     b_rows.rearrange("s n t -> (s n t)").rearrange("(c r) -> c r", r=NB * SEC)[c, :]
                                     .partition_broadcast(P)).then_inc(b_loaded, 16)
                    if "A" in stages:
                        if "D" in stages:
                            sp.wait_ge(r_done, past(p))
                        sp.wait_ge(x_loaded, 16 * (t + 1))
                        sp.dma_start(x_ring[:, (t + 1) % XR, :],
                                     x.rearrange("(t p) d -> t p d", p=P)[(t + 1) % NT, :, :])\
                            .then_inc(x_loaded, 16)
                    if "B" in stages:
                        b = t - 1
                        sp.wait_ge(xp_done, past(3 * (b + 1)))
                        sp.dma_start(b_rows[b // QT, :, tcol(b)], bt_tile[1:1 + NST, :]).then_inc(b_stored, 16)
                    if "D" in stages:
                        sp.wait_ge(x1_done, past(p + 1))
                        sp.dma_start(y_rows.rearrange("(t p) d -> t p d", p=P)[p, :, :],
                                     rows[:, 0, 0:DIM]).then_inc(y_stored, 16)

            sp.wait_ge(scattered, 32 * (NT + 1) + 16)
            sp.wait_ge(y_stored, 16 * NT + 16)
            for k in range(2):
                sp.dma_start(xg[:, k], slot_rows.rearrange("(e t p) c -> e p t c", p=P, t=ST)[k])\
                    .then_inc(xg_in[k], 16)
            load_expert(1, 1)
            with sp.Fori(1, EXPERTS // 2) as pair:
                e = 2 * pair
                for k in range(2):
                    sp.wait_ge(down_psum, past(ST * (e + k - 1)))
                    load_expert(e + k, k)
                    sp.wait_ge(eow_done, past(ST * (e + k - 1)))
                    sp.dma_start(xg[:, k], slot_rows.rearrange("(e t p) c -> e p t c", p=P, t=ST)[e + k])\
                        .then_inc(xg_in[k], 16)

            y_v = y_rows.rearrange("(s t p) d -> s p t d", p=P, t=FT)
            out_v = out.rearrange("(s t p) d -> s p t d", p=P, t=FT)
            sp.wait_ge(added, 16 * ST * EXPERTS + 16)
            for k in range(2):
                sp.dma_start(yt[:, k], y_v[k]).then_inc(yt_in[k], 16)
            for s in range(NT // FT):
                sp.wait_ge(fo_done, FT * (s + 1))
                sp.dma_start(out_v[s], yo[:, s % 2]).then_inc(out_st[s % 2], 16)
                if s + 2 < NT // FT:
                    sp.dma_start(yt[:, s % 2], y_v[s + 2]).then_inc(yt_in[s % 2], 16)
            sp.wait_ge(out_st[0], 16 * (NT // FT // 2))
            sp.wait_ge(out_st[1], 16 * (NT // FT // 2))

        @block.gpsimd
        def _(pool):
            pool.memset(ident[:, :], 0.0).then_inc(masks_made, 1)
            pool.memset(upper[:, :], 1.0).then_inc(masks_made, 1)
            pool.memset(ones[:, :], 1.0).then_inc(masks_made, 1)
            pool.iota(iota8[:, :], pattern=[[1, EXPERTS]], base=0, channel_multiplier=0,
                      allow_small_or_imprecise_dtypes=True).then_inc(masks_made, 1)
            pool.iota(token_no[:, :], pattern=[[P, NT]], base=0, channel_multiplier=1,
                      allow_small_or_imprecise_dtypes=True).then_inc(masks_made, 1)
            pool.wait_ge(masks_made, 5)
            pool.affine_select(out=ident[:, :], in_=ident[:, :], compare_op=ALU.not_equal, fill=1.0, base=0,
                               pattern=[[-1, P]], channel_multiplier=1).then_inc(masks_made, 1)
            pool.affine_select(out=upper[:, :], in_=upper[:, :], compare_op=ALU.is_gt, fill=0.0, base=0,
                               pattern=[[1, P]], channel_multiplier=-1).then_inc(masks_made, 1)
            pool.memset(zero[:, :], 0.0).then_inc(state_zeroed, 1)
            pool.memset(rows[:, :, :], 0.0).then_inc(state_zeroed, 1)
            pool.memset(slot[:, :], SLOTS).then_inc(state_zeroed, 1)
            pool.memset(gden[:, :], 1.0).then_inc(state_zeroed, 1)
            pool.memset(gtop[:, :], 0.0).then_inc(state_zeroed, 1)
            pool.memset(mhalf[:, :], -0.5).then_inc(masks_made, 1)
            pool.memset(xp0[:, :], 1.0).then_inc(state_zeroed, 1)
            pool.memset(halo[:, :, :, :], 0.0).then_inc(state_zeroed, 1)
            pool.memset(carry[:, :, :, :], 0.0).then_inc(state_zeroed, 1)
            pool.memset(taken[:, :], 0.0).then_inc(state_zeroed, 1)
            pool.memset(acc[:, :, :, :], 0.0).then_inc(state_zeroed, 1)
            pool.wait_ge(masks_made, 8)
            pool.wait_ge(empty_made, 2)
            pool.dma_start(slot_rows.rearrange("(t p) c -> p t c", p=P),
                           empty_row[:, :].rearrange("p (a c) -> p a c", a=1).to_broadcast([P, SLOTS // P, ROW]))\
                .then_inc(scattered, 16)

            def front_inverse_std(t):
                pool.wait_ge(mv1_done, t + 1)
                apart(pool)
                pool.tensor_scalar(veps[:, 0:1], mv[:, 0, 1:2], EPS, None, ALU.add).then_inc(veps1_done, 1)
                pool.wait_ge(veps1_done, t + 1)
                apart(pool)
                pool.tensor_tensor(rstd[:, 0:1], veps[:, 0:1], mhalf[:, 0:1], ALU.pow).then_inc(rstd1_done, 1)

            def back_inverse_std(p):
                pool.wait_ge(mv2_done, p + 1)
                apart(pool)
                pool.tensor_scalar(veps2[:, :], mv2[:, 1:2], EPS, None, ALU.add).then_inc(veps2_done, 1)
                pool.wait_ge(veps2_done, p + 1)
                apart(pool)
                pool.tensor_tensor(rstd2[:, :], veps2[:, :], mhalf[:, 0:1], ALU.pow).then_inc(rstd2_done, 1)

            def make_u(c, k):
                j, g = k // DG, k % DG
                if k == 0:
                    pool.wait_ge(dx_done, past(QT * (c // QT) + QT))
                    pool.wait_ge(b_loaded, 16 * (c + 1))
                pool.wait_ge(scans_done, STEPS * c + k - 3 + SCAN0)
                apart(pool)
                pool.tensor_tensor(u[:, k % 4, :], dx[:, (c // QT) % 2, g, :], b_bc[:, c % 2, j, :],
                                   ALU.mult).then_inc(u_ready, 1)

            def make_delta(b, c, scanning):
                pool.wait_ge(sprelu_done, past(b + 1))
                pool.wait_ge(spln_done, b + 1)
                if scanning:
                    pool.wait_ge(scans_done, STEPS * QT * (c // QT) + SCAN0)
                apart(pool)
                pool.tensor_tensor(delta[:, (b // QT) % 2, :, tcol(b)], sp_ln[:, :, :], sp_relu[:, :, :],
                                   ALU.add).then_inc(delta_done, 1)
                pool.wait_ge(delta_done, past(b + 1))
                apart(pool)
                pool.tensor_tensor(dx[:, (b // QT) % 2, :, tcol(b)], delta[:, (b // QT) % 2, :, tcol(b)],
                                   xc_tile[:, :, :], ALU.mult).then_inc(dx_done, 1)

            def dispatch(n):
                pool.wait_ge(slot_done, past(n))
                pool.wait_ge(gate_done, past(n + 1))
                pool.wait_ge(x1_copied, past(n))
                pool.wait_ge(ids_done, past(n))
                apart(pool)
                for k in range(2):
                    pool.indirect_dma_start(
                        slot_rows[:, :], bass.IndirectOffsetOnAxis(ap=slot[:, k:k + 1], axis=0),
                        rows[:, k, :], None, bounds_check=SLOTS - 1, oob_is_err=False).then_inc(scattered, 16)

            front_inverse_std(0)
            for first, last, stages in PHASES:
                with pool.Fori(first, last) as i:
                    t, c, p = i, i - LEAD, i - BACK
                    for k in range(STEPS):
                        if "C" in stages:
                            make_u(c, k)
                        if "D" in stages and k == 6:
                            dispatch(p)
                        if "A" in stages and k == 10:
                            front_inverse_std(t + 1)
                        if "D" in stages and k == 13:
                            back_inverse_std(p)
                    if "B" in stages:
                        make_delta(t - 1, c, "C" in stages)
                    if "D" in stages:
                        pool.wait_ge(scattered, 32 * (p + 1) + 16)
                        apart(pool)
                        pool.tensor_copy(rows[:, :, DIM + 1], token_no[:, bass.ds(p, 1)].to_broadcast([P, 2]))\
                            .then_inc(ids_done, 1)
            dispatch(NT)

            pool.wait_ge(scattered, 32 * (NT + 1) + 16)
            pool.wait_ge(y_stored, 16 * NT + 16)
            pool.dma_start(b2_bc[:, :, :].rearrange("p e d -> p (e d)"),
                           b2.rearrange("e d -> (e d)").partition_broadcast(P)).then_inc(added, 16)

            def add_rows(e, k):
                pool.wait_ge(added, 16 * ST * e + 16)
                pool.sem_inc(landed, 1)
                apart(pool)
                pool.wait_ge(gidx_done, e + 1)
                for t in range(ST):
                    pool.wait_ge(eow_done, past(ST * e + t + 1))
                    apart(pool)
                    pool.indirect_dma_start(
                        y_rows[:, :], bass.IndirectOffsetOnAxis(ap=gidx[:, k, t:t + 1], axis=0), eo_w[:, k, t, :],
                        None, bounds_check=TOK - 1, oob_is_err=False, compute_op=ALU.add).then_inc(added, 16)

            with pool.Fori(0, EXPERTS // 2) as pair:
                e = 2 * pair
                for k in range(2):
                    add_rows(e + k, k)

            for s in range(NT // FT):
                pool.wait_ge(fmv_done, FT * (s + 1))
                pool.tensor_scalar(veps[:, :], mv[:, :, 1], EPS, None, ALU.add).then_inc(fveps_done, 1)
                pool.wait_ge(fveps_done, s + 1)
                if s:
                    pool.wait_ge(fnmr_done, s)
                pool.tensor_tensor(rstd[:, :], veps[:, :], mhalf[:, :], ALU.pow).then_inc(frstd_done, 1)

        @block.scalar
        def _(act):
            for count, credit in ((scans_done, SCAN0), (u_ready, U0), (hT_psum, HT0), (acc_done, ACC0),
                                  (carry_saved, CARRY0), (acc_zeroed, ACCZ0), (gelu_done, GEL0), (eob_done, EOB0),
                                  (b_stored, 16), (y_stored, 16)):
                act.sem_inc(count, credit)
            for count in (xc_done, y_done, slot_done, ids_done, sz_done, yT_psum, z_psum, conv_psum, xi_done, dx_done, dt_psum, delta_done, gate_done, down_psum, xp_done, pos_done, lg_done, sprelu_done, xgT_done, xnT_psum, o_psum, x1_done, x1_copied, gexp_done, cnt_psum, taken_done, eow_done, landed, r_done):
                act.sem_inc(count, 1)
            act.wait_ge(small_in, 16 * 10)
            act.activation(aexp[:, :, :], alog_sb[:, :, :], ACT.Exp).then_inc(aexp_done, 1)
            act.wait_ge(aexp_done, 1)
            act.activation(nega[:, :, :].rearrange("p n g -> p g n"), aexp[:, :, :], ACT.Copy, scale=-1.0)\
                .then_inc(nega_done, 1)
            act.wait_ge(nega_done, 1)
            act.wait_ge(state_zeroed, 10)

            def decay(c, k):
                j, g = k // DG, k % DG
                if k == 0:
                    act.wait_ge(delta_done, past(QT * (c // QT) + QT))
                act.wait_ge(scans_done, STEPS * c + k - 1 + SCAN0)
                act.activation(decay_ps[k % 2], delta[:, (c // QT) % 2, g, :], ACT.Exp,
                               scale=nega[:, bass.ds((c % QT) * NB + j, 1), g]).then_inc(decay_ready, 1)

            def clear_acc(p):
                act.wait_ge(acct_done, p + 1)
                act.activation(acc[:, (p // QT) % 2, p % QT, :], zero[:, 0:1].to_broadcast([P, DI]), ACT.Copy)\
                    .then_inc(acc_zeroed, 1)

            def take_xnT(t):
                act.wait_ge(xnT_psum, past(t + 1))
                act.wait_ge(z_psum, past(t))
                for k in range(KD):
                    act.activation(xnT[:, k, :], front_a[:, k * P:(k + 1) * P], ACT.Identity,
                                   bias=nb_sb[:, k:k + 1], scale=nw_sb[:, k:k + 1]).then_inc(xnT_done, 1)

            def take_xi(t):
                act.wait_ge(xi_psum, t + 1)
                act.wait_ge(conv_psum, past(t))
                act.wait_ge(xi_done, past(2 * t))
                act.activation(xi[:, :, 0:TAPS - 1], halo[:, t // TPB, :, :], ACT.Copy).then_inc(halo_in, 1)
                ps = front_b.rearrange("p (g t) -> p g t", g=DG)
                act.activation(xi[:, :, TAPS - 1:], ps, ACT.Copy).then_inc(xi_done, 1)
                act.wait_ge(halo_in, t + 1)
                apart(act)
                act.activation(halo[:, t // TPB, :, :], ps[:, :, P - TAPS + 1:P], ACT.Copy).then_inc(xi_done, 1)

            def take_z_xc(t, back, p):
                act.wait_ge(z_psum, past(t + 1))
                if back:
                    act.wait_ge(y_done, past(p + 1))
                    act.wait_ge(yT_psum, past(p + 1))
                act.activation(sz[:, t % RT, :, :], front_a.rearrange("p (g t) -> p g t", g=DG),
                               ACT.Silu).then_inc(sz_done, 1)
                act.wait_ge(conv_psum, past(t + 1))
                act.wait_ge(dx_done, past(t))
                for g in range(DG):
                    act.activation(xc_tile[:, g, :], front_b[:, g * P:(g + 1) * P], ACT.Silu,
                                   bias=cb_sb[:, g:g + 1]).then_inc(xct_done, 1)
                act.wait_ge(xct_done, DG * (t + 1))
                apart(act)
                act.preload_act_table_set("natural_log_exp_and_others")
                act.activation(xc[:, t % RT, :, :], xc_tile[:, :, :], ACT.Copy).then_inc(xc_done, 1)

            def take_xp(t):
                act.wait_ge(xp_psum, t + 1)
                act.wait_ge(b_stored, 16 * t + 16)
                act.activation(bt_tile[:, :], front_a[0:1 + NST, 0:P], ACT.Copy).then_inc(xp_done, 1)
                act.wait_ge(dt_psum, past(t))
                act.activation(xp0[0:1, :], front_a[0:1, 0:P], ACT.Copy).then_inc(xp_done, 1)
                act.activation(c_sb[:, (t // QT) % 2, t % QT, :], front_a[:, P:P + NST], ACT.Copy)\
                    .then_inc(xp_done, 1)

            def softplus_part(b, n):
                v = front_b.rearrange("p (g t) -> p g t", g=DG)
                if n == 0:
                    act.wait_ge(dt_psum, past(b + 1))
                    act.wait_ge(delta_done, past(b))
                    act.activation(sp_abs[:, :, :], v, ACT.Abs).then_inc(spabs_done, 1)
                if n == 1:
                    act.activation(sp_relu[:, :, :], v, ACT.Relu).then_inc(sprelu_done, 1)
                if n == 2:
                    act.wait_ge(spabs_done, b + 1)
                    act.activation(sp_exp[:, :, :], sp_abs[:, :, :], ACT.Exp, scale=-1.0).then_inc(spexp_done, 1)
                if n == 3:
                    act.wait_ge(spexp_done, b + 1)
                    act.activation(sp_ln[:, :, :], sp_exp[:, :, :], ACT.Ln, bias=1.0).then_inc(spln_done, 1)

            def take_x1T(p):
                act.wait_ge(x1_done, past(p + 1))
                act.activation(rows[:, 1, 0:DIM], rows[:, 0, 0:DIM], ACT.Copy).then_inc(x1_copied, 1)
                act.wait_ge(x1T_psum, p + 1)
                act.activation(x1T[:, :, :].rearrange("p k t -> p (k t)"), back_a[:, 0:KD * P], ACT.Copy)\
                    .then_inc(x1T_done, 1)

            def gate_exps(p):
                act.wait_ge(negmax_done, p + 1)
                act.wait_ge(gate_done, past(p + 1))
                act.activation(gexp[:, :], logits[:, :], ACT.Exp, bias=negmax[:, 0:1], accum_out=gden[:, 0:1])\
                    .then_inc(gexp_done, 1)
                act.activation(gtop[:, :], top8[:, 0:2], ACT.Exp, bias=negmax[:, 0:1]).then_inc(gexp_done, 1)

            act.preload_act_table_set("natural_log_exp_and_others")
            for first, last, stages in PHASES:
                with act.Fori(first, last) as i:
                    t, c, p = i, i - LEAD, i - BACK
                    for k in range(STEPS):
                        if "C" in stages:
                            decay(c, k)
                        if "A" in stages and k == 1:
                            take_xnT(t)
                        if "A" in stages and k == 5:
                            take_xi(t)
                        if "B" in stages and k == 6:
                            if "C" in stages:
                                act.wait_ge(acc_done, QT * NST * (c // QT) + ACC0)
                            take_xp(t - 1)
                        if "D" in stages and k == 7:
                            clear_acc(p)
                        if "B" in stages and 9 <= k < 13:
                            softplus_part(t - 1, k - 9)
                    if "D" in stages:
                        take_x1T(p)
                    if "A" in stages:
                        take_z_xc(t, "D" in stages, p)
                    if "D" in stages:
                        gate_exps(p)

            def gelu(e, k):
                act.wait_ge(down_psum, past(ST * e))
                for m in range(HG):
                    act.wait_ge(up_psum, HG * e + m + 1)
                    pair = banks[:, 2 * (m % 2):2 * (m % 2) + 2, 0:HALF]
                    act.activation(hid[:, m, :].rearrange("p (a b) -> p a b", a=2), pair, ACT.Gelu,
                                   bias=b1_sb[:, e, m:m + 1]).then_inc(gelu_done, 1)

            act.wait_ge(scattered, 32 * (NT + 1) + 16)
            with act.Fori(0, EXPERTS // 2) as pair:
                e = 2 * pair
                for k in range(2):
                    gelu(e + k, k)

            for s in range(NT // FT):
                act.wait_ge(fnmr_done, s + 1)
                act.wait_ge(yt_in[s % 2], 16 * (s // 2 + 1))
                if s >= 2:
                    act.wait_ge(out_st[s % 2], 16 * (s // 2))
                for n in range(FT):
                    act.activation(yo[:, s % 2, n, :], yt[:, s % 2, n, :], ACT.Identity,
                                   bias=nmr[:, s % 2, n:n + 1], scale=rstd2x[:, s % 2, n:n + 1])\
                        .then_inc(fo_done, 1)

        @block.tensor
        def _(pe):
            pe.wait_ge(weights_in, 16 * 4)
            pe.wait_ge(small_in, 16 * 10)
            pe.wait_ge(masks_made, 8)
            pe.wait_ge(consts_made, 2 + DG * TAPS + DG)
            pe.wait_ge(state_zeroed, 10)

            def state_sums(c, k):
                j, tt = k // DG, k % DG
                if tt == 0:
                    pe.wait_ge(scans_done, STEPS * c + DG * (j + 1) + SCAN0)
                pe.wait_ge(acc_done, STEPS * c + k - 1 + ACC0)
                for g in range(DG):
                    mm = pe.transpose(hT_ps[k % 2][:, g * P:(g + 1) * P], h[:, j % 2, g, tt * P:(tt + 1) * P],
                                      ident[:, :])
                mm.then_inc(hT_psum, 1)

            def x_norm_T(t):
                pe.wait_ge(xn_done, t + 1)
                pe.wait_ge(sz_done, past(t))
                for k in range(KD):
                    mm = pe.transpose(front_a[:, k * P:(k + 1) * P], xn[:, k * P:(k + 1) * P], ident[:, :])
                mm.then_inc(xnT_psum, 1)

            def project_in(half, bank, m):
                for k in range(KD):
                    mm = pe.matmul(bank[:, m * P:(m + 1) * P],
                                   in_sb[:, k, half * DI + m * P:half * DI + (m + 1) * P], xnT[:, k, :],
                                   start=(k == 0), stop=(k == KD - 1))
                return mm

            def convolve(g):
                for j in range(TAPS):
                    mm = pe.matmul(front_b[:, g * P:(g + 1) * P], conv_diag[:, g, j, :], xi[:, g, j:j + P],
                                   start=(j == 0), stop=(j == TAPS - 1))
                return mm

            def project_x(b):
                pe.wait_ge(xnT_done, KD * (b + 1))
                pe.wait_ge(xct_done, DG * (b + 1))
                for g in range(DG):
                    pe.matmul(front_a[0:1 + NST, 0:P], xp_sb[:, g, 0:1 + NST], xc_tile[:, g, :],
                              start=(g == 0), stop=(g == DG - 1))
                for g in range(DG):
                    mm = pe.matmul(front_a[:, P:P + NST], xc_tile[:, g, :], xp_sb[:, g, 1 + NST:],
                                   start=(g == 0), stop=(g == DG - 1))
                mm.then_inc(xp_psum, 1)

            def project_dt(t):
                pe.wait_ge(xp_done, past(3 * (t + 1)))
                for g in range(DG):
                    mm = pe.matmul(front_b[:, g * P:(g + 1) * P], dt_sb[:, g * P:(g + 1) * P], xp0[:, :],
                                   start=True, stop=True)
                mm.then_inc(dt_psum, 1)

            def y_channels(p):
                pe.wait_ge(acct_done, p + 1)
                pe.wait_ge(pos_done, past(2 * p))
                for g in range(DG):
                    pe.matmul(back_a[:, g * P:(g + 1) * P], acc_tile[:, g * P:(g + 1) * P], ident[:, :],
                              start=True, stop=False)
                    mm = pe.matmul(back_a[:, g * P:(g + 1) * P], skip_diag[:, g, :],
                                   xc[:, p % RT, g, :], start=False, stop=True)
                mm.then_inc(yT_psum, 1)

            def project_out(p, g0, g1):
                for g in range(g0, g1):
                    mm = pe.matmul(back_b[:, 0:DIM], y_tile[:, g, :], out_sb[:, g, :],
                                   start=(g == 0), stop=(g == DG - 1))
                return mm

            def x1_T(p):
                pe.wait_ge(x1_done, past(p + 1))
                for k in range(KD):
                    mm = pe.transpose(back_a[:, k * P:(k + 1) * P], rows[:, 0, k * P:(k + 1) * P], ident[:, :])
                mm.then_inc(x1T_psum, 1)

            def route(p):
                pe.wait_ge(x1T_done, p + 1)
                pe.wait_ge(r_done, past(p + 1))
                for k in range(KD):
                    mm = pe.matmul(back_b[:, 0:EXPERTS], x1T[:, k, :], rw_sb[:, k, :],
                                   start=(k == 0), stop=(k == KD - 1))
                mm.then_inc(lg_psum, 1)

            def count(p):
                pe.wait_ge(mask_done, p + 1)
                pe.matmul(back_a[:, 0:EXPERTS], upper_b[:, :], mask_b[:, :], start=True, stop=True)
                pe.matmul(back_a[:, EXPERTS:2 * EXPERTS], ones_b[:, :], mask_b[:, :], start=True, stop=True)\
                    .then_inc(cnt_psum, 1)

            for first, last, stages in PHASES:
                with pe.Fori(first, last) as i:
                    t, c, p = i, i - LEAD, i - BACK
                    if "A" in stages:
                        x_norm_T(t)
                    if "D" in stages:
                        y_channels(p)
                    if "A" in stages:
                        pe.wait_ge(xnT_done, KD * (t + 1))
                        pe.wait_ge(xc_done, past(t))
                        for m in range(DG):
                            mm = project_in(0, front_b, m)
                        mm.then_inc(xi_psum, 1)
                    for k in range(STEPS):
                        if "C" in stages:
                            state_sums(c, k)
                        if "B" in stages and k == 1:
                            if "A" in stages:
                                pe.wait_ge(xnT_done, KD * (t + 1))
                            project_x(t - 1)
                        if "D" in stages and k == 2:
                            pe.wait_ge(y_done, past(p + 1))
                            pe.wait_ge(lg_done, past(p))
                            project_out(p, 0, 2)
                        if "D" in stages and k == 3:
                            project_out(p, 2, DG).then_inc(o_psum, 1)
                        if "B" in stages and k == 4:
                            if "A" in stages:
                                pe.wait_ge(xi_done, past(2 * (t + 1)))
                            project_dt(t - 1)
                        if "A" in stages and k == 6:
                            if "B" in stages:
                                pe.wait_ge(xp_done, past(3 * t))
                            project_in(1, front_a, 0)
                            project_in(1, front_a, 1)
                        if "A" in stages and k == 7:
                            project_in(1, front_a, 2)
                            project_in(1, front_a, 3).then_inc(z_psum, 1)
                        if "A" in stages and k == 8:
                            pe.wait_ge(xi_done, past(2 * (t + 1)))
                            if "B" in stages:
                                pe.wait_ge(sprelu_done, past(t))
                            convolve(0)
                        if "A" in stages and k in (9, 10):
                            convolve(k - 8)
                        if "A" in stages and k == 11:
                            convolve(3).then_inc(conv_psum, 1)
                        if "D" in stages and k == 9:
                            x1_T(p)
                        if "D" in stages and k == 12:
                            route(p)
                        if "D" in stages and k == 14:
                            count(p)

            def gathered_T(e, k, kd):
                if kd == 0:
                    pe.wait_ge(xg_in[k], 8 * (e - k) + 16)
                pe.wait_ge(xgT_done, past(KD * e + kd))
                for t in range(ST):
                    mm = pe.transpose(banks[:, 6:8, :].rearrange("p a b -> p (a b)")[:, t * P:(t + 1) * P],
                                      xg[:, k, t, kd * P:(kd + 1) * P], ident[:, :])
                mm.then_inc(xgT_psum, 1)

            def expert(e, k, following):
                pe.wait_ge(w_in[k], 16 * (e - k) + 32)
                pe.wait_ge(xgT_done, past(KD * (e + 1)))
                for m in range(HG):
                    pe.wait_ge(gelu_done, HG * e + m - 1 + GEL0)
                    for a in range(2):
                        for kd in range(KD):
                            mm = pe.matmul(banks[:, 2 * (m % 2) + a, 0:HALF], w1_sb[k][:, kd, m * P:(m + 1) * P],
                                           xgT[:, k, kd, a * HALF:(a + 1) * HALF],
                                           start=(kd == 0), stop=(kd == KD - 1))
                    mm.then_inc(up_psum, 1)
                    if following and m in (3, 7):
                        gathered_T(e + 1, 1 - k, m // 4)
                pe.wait_ge(gelu_done, HG * (e + 1) + GEL0)
                for t in range(ST):
                    pe.wait_ge(eob_done, ST * e + t - 1 + EOB0)
                    for m in range(HG):
                        mm = pe.matmul(banks[:, 4 + (ST * k + t) % 2, 0:DIM], hid[:, m, t * P:(t + 1) * P],
                                       w2_sb[k][:, m, :], start=(m == 0), stop=(m == HG - 1))
                    mm.then_inc(down_psum, 1)

            pe.wait_ge(scattered, 32 * (NT + 1) + 16)
            gathered_T(0, 0, 0)
            gathered_T(0, 0, 1)
            with pe.Fori(0, EXPERTS // 2 - 1) as pair:
                e = 2 * pair
                expert(e, 0, True)
                expert(e + 1, 1, True)
            expert(EXPERTS - 2, 0, True)
            expert(EXPERTS - 1, 1, False)

        @block.vector
        def _(dve):
            dve.memset(empty_row[:, 0:ROW - 1], 0.0).then_inc(empty_made, 1)
            dve.memset(empty_row[:, ROW - 1:ROW], FAR).then_inc(empty_made, 1)
            dve.wait_ge(masks_made, 8)
            dve.wait_ge(small_in, 16 * 10)
            dve.tensor_copy(ones_b[:, :], ones[:, :]).then_inc(consts_made, 1)
            dve.tensor_copy(upper_b[:, :], upper[:, :]).then_inc(consts_made, 1)
            for g in range(DG):
                for j in range(TAPS):
                    dve.tensor_scalar(conv_diag[:, g, j, :], ident[:, :], cw_sb[:, g, j:j + 1], None, ALU.mult)\
                        .then_inc(consts_made, 1)
            for g in range(DG):
                dve.tensor_scalar(skip_diag[:, g, :], ident[:, :], ds_sb[:, g:g + 1], None, ALU.mult)\
                    .then_inc(consts_made, 1)
            dve.wait_ge(state_zeroed, 10)

            def scan_step(c, k):
                j, g = k // DG, k % DG
                if g == 0:
                    dve.wait_ge(hT_psum, DG * (NB * c + j) - 4 + HT0)
                    dve.wait_ge(carry_saved, NB * c + j - 1 + CARRY0)
                dve.wait_ge(u_ready, STEPS * c + k + 1 + U0)
                dve.wait_ge(decay_ready, STEPS * c + k + 1)
                dve.tensor_tensor_scan(h[:, j % 2, g, :], decay_ps[k % 2], u[:, k % 4, :],
                                       carry[:, c // TPB, bass.ds((c % QT) * NB + j, 1), g],
                                       ALU.mult, ALU.add).then_inc(scans_done, 1)

            def save_carry(c, j):
                dve.wait_ge(scans_done, STEPS * c + DG * (j + 1) + SCAN0)
                apart(dve)
                dve.tensor_copy(carry[:, c // TPB, bass.ds((c % QT) * NB + j, 1), :]
                                .rearrange("p a g -> p (a g)"), h[:, j % 2, :, SEC - 1])\
                    .then_inc(carry_saved, 1)

            def add_state(c, k):
                j, tt = k // DG, k % DG
                n = STEPS * c + k
                if k == 0:
                    dve.wait_ge(acc_zeroed, QT * (c // QT) - QT + ACCZ0)
                    dve.wait_ge(xp_done, past(3 * QT * (c // QT) + 3 * QT))
                dve.wait_ge(hT_psum, n + 1 + HT0)
                dve.wait_ge(acc_done, n - 3 + ACC0)
                a = acc[:, (c // QT) % 2, tt, :]
                dve.scalar_tensor_tensor(out=a, in0=hT_ps[tt % 2],
                                         scalar=c_sb[:, (c // QT) % 2, tt, bass.ds((c % QT) * NB + j, 1)],
                                         in1=a, op0=ALU.mult, op1=ALU.add).then_inc(acc_done, 1)

            def take_acc(p):
                dve.wait_ge(acc_done, QT * NST * (p // QT) + QT * NST + ACC0)
                dve.wait_ge(yT_psum, past(p))
                apart(dve)
                dve.tensor_copy(acc_tile[:, :], acc[:, (p // QT) % 2, p % QT, :]).then_inc(acct_done, 1)

            def front_stats(t):
                dve.wait_ge(x_loaded, 16 * (t + 1))
                dve.bn_stats(stat[:, 0, :], x_ring[:, t % XR, :]).then_inc(st1_done, 1)
                dve.wait_ge(st1_done, t + 1)
                apart(dve)
                dve.bn_aggr(mv[:, 0, :], stat[:, 0, :]).then_inc(mv1_done, 1)

            def front_norm(t):
                dve.wait_ge(rstd1_done, t + 1)
                dve.wait_ge(xnT_psum, past(t))
                dve.tensor_scalar(xn[:, :], x_ring[:, t % XR, :], mv[:, 0, 0:1], rstd[:, 0:1],
                                  ALU.subtract, ALU.mult).then_inc(xn_done, 1)

            def gate_y(p):
                dve.wait_ge(yT_psum, past(p + 1))
                dve.wait_ge(o_psum, past(p))
                dve.tensor_tensor(y_tile[:, :, :], back_a.rearrange("p (g t) -> p g t", g=DG),
                                  sz[:, p % RT, :, :], ALU.mult).then_inc(y_done, 1)

            def residual(p):
                dve.wait_ge(o_psum, past(p + 1))
                dve.wait_ge(x1_done, past(p))
                dve.scalar_tensor_tensor(out=r_tile[:, :], in0=x_ring[:, p % XR, :], scalar=2.0,
                                         in1=back_b[:, 0:DIM], op0=ALU.mult, op1=ALU.add)\
                    .then_inc(r_done, 1)
                dve.wait_ge(r_done, past(p + 1))
                dve.bn_stats(stat2[:, :], r_tile[:, :]).then_inc(st2_done, 1)
                dve.wait_ge(st2_done, p + 1)
                apart(dve)
                dve.bn_aggr(mv2[:, :], stat2[:, :]).then_inc(mv2_done, 1)

            def norm_x1(p):
                dve.wait_ge(rstd2_done, p + 1)
                dve.wait_ge(y_stored, 16 * p + 16)
                dve.wait_ge(scattered, 32 * (p + 1) + 16)
                dve.wait_ge(x1_copied, past(p))
                dve.tensor_scalar(rows[:, 0, 0:DIM], r_tile[:, :], mv2[:, 0:1], rstd2[:, 0:1],
                                  ALU.subtract, ALU.mult).then_inc(x1_done, 1)

            def choose(p):
                dve.wait_ge(lg_psum, p + 1)
                dve.wait_ge(gexp_done, past(2 * p))
                dve.tensor_tensor(logits[:, :], back_b[:, 0:EXPERTS], rb_sb[:, :], ALU.add)\
                    .then_inc(lg_done, 1)
                dve.wait_ge(lg_done, past(p + 1))
                apart(dve)
                dve.max(top8[:, :], logits[:, :]).then_inc(top_done, 1)
                dve.wait_ge(top_done, p + 1)
                apart(dve)
                dve.max_index(idx8[:, :], top8[:, :], logits[:, :]).then_inc(idx_done, 1)
                dve.tensor_scalar(negmax[:, :], top8[:, 0:1], -1.0, None, ALU.mult).then_inc(negmax_done, 1)
                dve.wait_ge(idx_done, p + 1)
                dve.tensor_copy(idxf[:, :], idx8[:, 0:2]).then_inc(idxf_done, 1)
                dve.wait_ge(idxf_done, p + 1)
                for k in range(2):
                    dve.tensor_scalar(choice[:, k, :], iota8[:, :], idxf[:, k:k + 1], None, ALU.is_equal)\
                        .then_inc(choice_done, 1)
                dve.wait_ge(choice_done, 2 * (p + 1))
                dve.wait_ge(cnt_psum, past(p))
                dve.tensor_tensor(mask_b[:, :], choice[:, 0, :], choice[:, 1, :], ALU.add)\
                    .then_inc(mask_done, 1)

            def gate_weights(n):
                dve.wait_ge(gexp_done, past(2 * n))
                dve.wait_ge(scattered, 32 * n + 16)
                dve.reciprocal(grec[:, :], gden[:, :]).then_inc(grec_done, 1)
                dve.wait_ge(grec_done, n + 1)
                dve.tensor_scalar(rows[:, :, DIM], gtop[:, :], grec[:, 0:1], None, ALU.mult)\
                    .then_inc(gate_done, 1)

            def place(p):
                dve.wait_ge(cnt_psum, past(p + 1))
                dve.wait_ge(taken_done, past(p))
                dve.tensor_tensor(pos[:, :], back_a[:, 0:EXPERTS], taken[:, :], ALU.add)\
                    .then_inc(pos_done, 1)
                dve.wait_ge(pos_done, past(2 * p + 1))
                dve.tensor_tensor(taken[:, :], back_a[:, EXPERTS:2 * EXPERTS], taken[:, :], ALU.add)\
                    .then_inc(pos_done, 1)
                dve.wait_ge(pos_done, past(2 * p + 2))
                dve.tensor_tensor(pick[:, :, :], choice[:, :, :],
                                  pos[:, :].rearrange("p (a e) -> p a e", a=1).to_broadcast([P, 2, EXPERTS]),
                                  ALU.mult).then_inc(taken_done, 1)
                dve.wait_ge(taken_done, past(p + 1))
                dve.tensor_reduce(posk[:, :], pick[:, :, :], mybir.AxisListType.X, ALU.add)\
                    .then_inc(pick_done, 1)
                dve.wait_ge(pick_done, p + 1)
                dve.scalar_tensor_tensor(out=slotf[:, :], in0=idxf[:, :], scalar=float(CAP), in1=posk[:, :],
                                         op0=ALU.mult, op1=ALU.add).then_inc(slotf_done, 1)
                dve.tensor_scalar(over[:, :], posk[:, :], float(CAP), FAR, ALU.is_ge, ALU.mult)\
                    .then_inc(over_done, 1)
                dve.wait_ge(slotf_done, p + 1)
                dve.wait_ge(over_done, p + 1)
                dve.tensor_tensor(slot[:, :], slotf[:, :], over[:, :], ALU.add).then_inc(slot_done, 1)

            front_stats(0)
            front_norm(0)
            for first, last, stages in PHASES:
                with dve.Fori(first, last) as i:
                    t, c, p = i, i - LEAD, i - BACK
                    if "D" in stages:
                        take_acc(p)
                    for k in range(STEPS):
                        if "C" in stages:
                            scan_step(c, k)
                            if k >= LAG:
                                add_state(c, k - LAG)
                            if k >= DG and k % DG == 0:
                                save_carry(c, k // DG - 1)
                        if "D" in stages and k == 1:
                            gate_weights(p)
                        if "D" in stages and k == 5:
                            gate_y(p)
                        if "A" in stages and k == 6:
                            front_stats(t + 1)
                        if "D" in stages and k == 9:
                            residual(p)
                        if "A" in stages and k == 10:
                            front_norm(t + 1)
                        if "D" in stages and k == 12:
                            norm_x1(p)
                    if "C" in stages:
                        add_state(c, STEPS - LAG)
                        save_carry(c, NB - 1)
                        add_state(c, STEPS - LAG + 1)
                    if "D" in stages:
                        choose(p)
                    if "C" in stages:
                        for n in range(STEPS - LAG + 2, STEPS):
                            add_state(c, n)
                    if "D" in stages:
                        place(p)
            gate_weights(NT)

            def take_gathered(e, k):
                dve.wait_ge(xg_in[k], 8 * (e - k) + 16)
                dve.wait_ge(landed, past(e))
                dve.tensor_copy(gidx[:, k, :], xg[:, k, :, ROW - 1]).then_inc(gidx_done, 1)
                for kd in range(KD):
                    dve.wait_ge(xgT_psum, KD * e + kd + 1)
                    dve.tensor_copy(xgT[:, k, kd, :],
                                    banks[:, 6:8, :].rearrange("p a b -> p (a b)")[:, 0:CAP])\
                        .then_inc(xgT_done, 1)

            def weigh(e, k, following):
                if following:
                    take_gathered(e + 1, 1 - k)
                dve.wait_ge(landed, past(e))
                dve.wait_ge(eow_done, past(ST * e))
                for t in range(ST):
                    dve.wait_ge(down_psum, past(ST * e + t + 1))
                    dve.tensor_tensor(eo[:, t, :], banks[:, 4 + (ST * k + t) % 2, 0:DIM], b2_bc[:, e, :],
                                      ALU.add).then_inc(eob_done, 1)
                    dve.wait_ge(eob_done, ST * e + t + 1 + EOB0)
                    dve.tensor_scalar(eo_w[:, k, t, :], eo[:, t, :], xg[:, k, t, DIM:DIM + 1], None, ALU.mult)\
                        .then_inc(eow_done, 1)

            dve.wait_ge(added, 16)
            take_gathered(0, 0)
            with dve.Fori(0, EXPERTS // 2 - 1) as pair:
                e = 2 * pair
                weigh(e, 0, True)
                weigh(e + 1, 1, True)
            weigh(EXPERTS - 2, 0, True)
            weigh(EXPERTS - 1, 1, False)

            for s in range(NT // FT):
                dve.wait_ge(yt_in[s % 2], 16 * (s // 2 + 1))
                if s:
                    dve.wait_ge(fnmr_done, s)
                for n in range(FT):
                    dve.bn_stats(stat[:, n, :], yt[:, s % 2, n, :]).then_inc(fst_done, 1)
                for n in range(FT):
                    dve.wait_ge(fst_done, FT * s + n + 1)
                    dve.bn_aggr(mv[:, n, :], stat[:, n, :]).then_inc(fmv_done, 1)
                dve.wait_ge(frstd_done, s + 1)
                if s >= 2:
                    dve.wait_ge(fo_done, FT * (s - 1))
                dve.tensor_copy(rstd2x[:, s % 2, :], rstd[:, :]).then_inc(fr_copied, 1)
                dve.wait_ge(fr_copied, s + 1)
                dve.scalar_tensor_tensor(out=nmr[:, s % 2, :], in0=mv[:, :, 0], scalar=-1.0, in1=rstd[:, :],
                                         op0=ALU.mult, op1=ALU.mult).then_inc(fnmr_done, 1)


_INS = ["x", "norm_w", "norm_b", "in_proj_w", "conv_w", "conv_b", "x_proj_w", "dt_w", "dt_b", "A_log", "D_skip",
        "out_proj_w", "router_w", "router_b", "w1", "b1", "w2", "b2"]


def kernel(**inputs):
    import numpy as _np
    import concourse.bacc as _bacc
    from concourse import mybir as _mybir
    from concourse.bass_utils import run_bass_kernel_spmd as _run

    nc = _bacc.Bacc("TRN2", target_bir_lowering=False, num_devices=1)
    arrays, args = {}, []
    for name in _INS:
        part = "L0_ffn_" if name in ("router_w", "router_b", "w1", "b1", "w2", "b2") else "L0_attn_"
        a = _np.asarray(inputs[part + name])
        if name == "x":
            a = a.reshape(-1, a.shape[-1])
        if name in ("in_proj_w", "x_proj_w", "out_proj_w"):
            a = a.T
        if name in ("norm_w", "norm_b", "conv_b", "D_skip"):
            a = a.reshape(-1, P).T
        if name == "dt_w":
            a = a.T
        if name == "b1":
            a = a.reshape(EXPERTS, HG, P).transpose(2, 0, 1)
        a = _np.ascontiguousarray(a)
        arrays[f"in_{name}_dram"] = a
        args.append(nc.dram_tensor(f"in_{name}_dram", a.shape, _mybir.dt.from_np(a.dtype), kind="ExternalInput").ap())
    out = nc.dram_tensor("out_0_dram", (TOK, DIM), F32, kind="ExternalOutput").ap()
    build(nc, *args, out)
    r = _run(nc, [arrays], core_ids=[0])
    return r.results[0]["out_0_dram"].reshape(BATCH, SEQ, DIM)
```

```python
from contextlib import ExitStack

import concourse.bass as bass
from concourse import mybir

F32 = mybir.dt.float32
BF16 = mybir.dt.bfloat16
U32 = mybir.dt.uint32
ALU = mybir.AluOpType
ACT = mybir.ActivationFunctionType

P = 128
DIM = 256
DI = 512
DG = DI // P
KD = DIM // P
NST = 16
TAPS = 4
BATCH, SEQ = 2, 2048
TOK = BATCH * SEQ
NT = TOK // P
SEC = 512
QT = SEC // P
NB = NST // QT
STEPS = NB * DG
TPB = SEQ // P
XR = 12
EXPERTS, HID, CAP = 8, 1024, 640
SLOTS = EXPERTS * CAP
ST = CAP // P
HG = HID // P
HALF = CAP // 2
ROW = DIM + 2
EPS = 1e-5
FAR = 1.0e6
LEAD = QT + 2
BACK = LEAD + QT
FULL = -(-(BACK + 2) // QT) * QT
RT = 10
LAG = 5
FT = 4

SCAN0 = STEPS
U0 = 2 * STEPS
HT0 = 4
ACC0 = 4
CARRY0 = NST
ACCZ0 = QT
GEL0 = 2
EOB0 = 2


def number(tile):
    return tile.section * QT + tile.within if isinstance(tile, Tile) else tile


def past(n):
    return number(n) + 1


class Tile:

    def __init__(self, section, within):
        self.section = section + within // QT if within // QT else section
        self.within = within % QT

    def __add__(self, n):
        return Tile(self.section, self.within + n)

    def __sub__(self, n):
        return Tile(self.section, self.within - n)

    def __rmul__(self, n):
        return self.section * (QT * n) + self.within * n

    def __floordiv__(self, n):
        return self.section if n == QT else self.section // (n // QT)

    def __mod__(self, n):
        return self.within if n == QT else (QT * self.section + self.within) % n


def build(nc, x, norm_w, norm_b, in_w, conv_w, conv_b, xp_w, dt_w, dt_b, a_log, d_skip, out_w,
          router_w, router_b, w1, b1, w2, b2, out):
    with ExitStack() as ctx:
        scope = [ctx]

        def sb(name, shape, dt=F32):
            return scope[0].enter_context(nc.sbuf_tensor(name, shape, dt))

        def sem(name):
            return ctx.enter_context(nc.semaphore(name))

        b_rows = nc.dram_tensor("b_rows", [NT // QT, NST, SEC], F32, kind="Internal").ap()
        slot_rows = nc.dram_tensor("slot_rows", [SLOTS, ROW], F32, kind="Internal").ap()
        y_rows = nc.dram_tensor("y_rows", [TOK, DIM], F32, kind="Internal").ap()

        banks = ctx.enter_context(nc.psum_tensor("banks", [P, 8, 512], F32))
        hT_ps = [banks[:, 2, :], banks[:, 3, :]]
        front_a, front_b = banks[:, 4, :], banks[:, 5, :]
        back_a, back_b = banks[:, 6, :], banks[:, 7, :]

        ident = sb("ident", [P, P])
        w1_sb = [sb("w1_even", [P, KD, HID])]
        b1_sb = sb("b1_sb", [P, EXPERTS, HG])
        mhalf = sb("mhalf", [P, FT])
        stat = sb("stat", [P, 6])
        mv = sb("mv", [P, 2])
        veps = sb("veps", [P, 1])
        rstd = sb("rstd", [P, 1])

        ssm = ExitStack()
        scope[0] = ssm
        in_sb = sb("in_sb", [P, KD, 2 * DI])
        out_sb = sb("out_sb", [P, DG, DIM])
        xp_sb = sb("xp_sb", [P, DG, 1 + 2 * NST])
        rw_sb = sb("rw_sb", [P, KD, EXPERTS])
        rb_sb = sb("rb_sb", [P, EXPERTS])
        nw_sb = sb("nw_sb", [P, KD])
        nb_sb = sb("nb_sb", [P, KD])
        cw_sb = sb("cw_sb", [P, DG, TAPS])
        cb_sb = sb("cb_sb", [P, DG])
        ds_sb = sb("ds_sb", [P, DG])
        dt_sb = sb("dt_sb", [2, DI])
        alog_sb = sb("alog_sb", [P, DG, NST])
        aexp = sb("aexp", [P, DG, NST])
        nega = sb("nega", [P, NST, DG])
        conv_diag = sb("conv_diag", [P, DG, TAPS, P])
        skip_diag = sb("skip_diag", [P, DG, P])
        ones = sb("ones", [P, P])
        zero = sb("zero", [P, 1])
        eps = sb("eps", [P, 1])
        ones_b = sb("ones_b", [P, P], BF16)
        upper = sb("upper", [P, P])
        upper_b = sb("upper_b", [P, P], BF16)
        iota8 = sb("iota8", [P, EXPERTS])
        token_no = sb("token_no", [P, NT])
        empty_row = sb("empty_row", [P, ROW])

        x_ring = sb("x_ring", [P, XR, DIM])
        xn = sb("xn", [P, DIM])
        xnT = sb("xnT", [P, KD, P])
        xi = sb("xi", [P, DG, TAPS - 1 + P])
        halo = sb("halo", [P, BATCH, DG, TAPS - 1])
        xc_tile = sb("xc_tile", [P, DG, P])
        xc = sb("xc", [P, RT, DG, P])
        sz = sb("sz", [P, RT, DG, P])
        bt_tile = sb("bt_tile", [1 + NST, P])
        xp0 = sb("xp0", [2, P])
        c_sb = sb("c_sb", [P, 3, QT, NST])
        sp_ln = sb("sp_ln", [P, DG, P])
        sp_relu = sb("sp_relu", [P, DG, P])
        delta = sb("delta", [P, 2, DG, SEC])
        dx = sb("dx", [P, 2, DG, SEC])
        b_bc = sb("b_bc", [P, 2, NB, SEC])
        u = sb("u", [P, 4, SEC])
        decay_sb = sb("decay_sb", [P, 2, SEC])
        decays = [banks[:, 0, :], decay_sb[:, 0, :], banks[:, 1, :], decay_sb[:, 1, :]]
        h = sb("h", [P, 2, DG, SEC])
        carry = sb("carry", [P, BATCH, NST, DG])
        acc = sb("acc", [P, 2, QT, DI])
        acc_tile = sb("acc_tile", [P, DI])
        y_tile = sb("y_tile", [P, DG, P])
        r_tile = sb("r_tile", [P, DIM])
        stat2 = sb("stat2", [P, 6])
        mv2 = sb("mv2", [P, 2])
        veps2 = sb("veps2", [P, 1])
        rstd2 = sb("rstd2", [P, 1])
        x1_tile = sb("x1_tile", [P, DIM])
        rows = sb("rows", [P, 2, ROW])
        x1T = sb("x1T", [P, KD, P])
        logits = sb("logits", [P, EXPERTS])
        top8 = sb("top8", [P, 8])
        idx8 = sb("idx8", [P, 8], U32)
        idxf = sb("idxf", [P, 2])
        choice = sb("choice", [P, 2, EXPERTS])
        mask_b = sb("mask_b", [P, EXPERTS], BF16)
        negmax = sb("negmax", [P, 1])
        gexp = sb("gexp", [P, EXPERTS])
        gden = sb("gden", [P, 1])
        gtop = sb("gtop", [P, 2])
        grec = sb("grec", [P, 1])
        taken = sb("taken", [P, EXPERTS])
        pos = sb("pos", [P, EXPERTS])
        pick = sb("pick", [P, 2, EXPERTS])
        posk = sb("posk", [P, 2])
        slotf = sb("slotf", [P, 2])
        over = sb("over", [P, 2])
        slot = sb("slot", [P, 2], U32)
        ssm.close()

        ffn = ExitStack()
        ctx.enter_context(ffn)
        scope[0] = ffn
        w1_sb.append(sb("w1_odd", [P, KD, HID]))
        w2_sb = [sb("w2_even", [P, HG, DIM]), sb("w2_odd", [P, HG, DIM])]
        xg = sb("xg", [P, 2, ST, ROW])
        gidx = sb("gidx", [P, 2, ST], U32)
        xgT = sb("xgT", [P, 2, KD, CAP])
        hid = sb("hid", [P, HG, CAP])
        b2_bc = sb("b2_bc", [P, EXPERTS, DIM])
        eo = sb("eo", [P, ST, DIM])
        eo_w = sb("eo_w", [P, 2, ST, DIM])
        yt = sb("yt", [P, NT, DIM])
        yo = sb("yo", [P, NT, DIM])
        fstat = sb("fstat", [P, NT, 6])
        fmv = sb("fmv", [P, NT, 2])
        fveps = sb("fveps", [P, NT])
        frstd = sb("frstd", [P, NT])
        nmr = sb("nmr", [P, NT])

        in_proj_in = sem("in_proj_in")
        weights_in = sem("weights_in")
        small_in = sem("small_in")
        x_loaded = sem("x_loaded")
        masks_made = sem("masks_made")
        consts_made = sem("consts_made")
        empty_made = sem("empty_made")
        state_zeroed = sem("state_zeroed")
        aexp_done = sem("aexp_done")
        nega_done = sem("nega_done")
        st1_done = sem("st1_done")
        mv1_done = sem("mv1_done")
        veps1_done = sem("veps1_done")
        rstd1_done = sem("rstd1_done")
        xn_done = sem("xn_done")
        xnT_psum = sem("xnT_psum")
        xnT_done = sem("xnT_done")
        xi_psum = sem("xi_psum")
        z_psum = sem("z_psum")
        halo_in = sem("halo_in")
        xi_done = sem("xi_done")
        conv_psum = sem("conv_psum")
        sz_done = sem("sz_done")
        xct_done = sem("xct_done")
        xc_done = sem("xc_done")
        xp_psum = sem("xp_psum")
        xp_done = sem("xp_done")
        b_stored = sem("b_stored")
        b_loaded = sem("b_loaded")
        dt_psum = sem("dt_psum")
        spabs_done = sem("spabs_done")
        spexp_done = sem("spexp_done")
        spln_done = sem("spln_done")
        sprelu_done = sem("sprelu_done")
        delta_done = sem("delta_done")
        dx_done = sem("dx_done")
        u_ready = sem("u_ready")
        decay_ready = sem("decay_ready")
        scans_done = sem("scans_done")
        carry_saved = sem("carry_saved")
        hT_psum = sem("hT_psum")
        acc_done = sem("acc_done")
        acct_done = sem("acct_done")
        acc_zeroed = sem("acc_zeroed")
        yT_psum = sem("yT_psum")
        y_done = sem("y_done")
        o_psum = sem("o_psum")
        r_done = sem("r_done")
        st2_done = sem("st2_done")
        mv2_done = sem("mv2_done")
        veps2_done = sem("veps2_done")
        rstd2_done = sem("rstd2_done")
        x1_done = sem("x1_done")
        x1_copied = sem("x1_copied")
        y_stored = sem("y_stored")
        ids_done = sem("ids_done")
        x1T_psum = sem("x1T_psum")
        x1T_done = sem("x1T_done")
        lg_psum = sem("lg_psum")
        lg_done = sem("lg_done")
        top_done = sem("top_done")
        idx_done = sem("idx_done")
        idxf_done = sem("idxf_done")
        choice_done = sem("choice_done")
        mask_done = sem("mask_done")
        negmax_done = sem("negmax_done")
        gexp_done = sem("gexp_done")
        grec_done = sem("grec_done")
        gate_done = sem("gate_done")
        cnt_psum = sem("cnt_psum")
        pos_done = sem("pos_done")
        taken_done = sem("taken_done")
        pick_done = sem("pick_done")
        slotf_done = sem("slotf_done")
        over_done = sem("over_done")
        slot_done = sem("slot_done")
        scattered = sem("scattered")
        gidx_done = sem("gidx_done")
        xgT_psum = sem("xgT_psum")
        xgT_done = sem("xgT_done")
        up_psum = sem("up_psum")
        gelu_done = sem("gelu_done")
        down_psum = sem("down_psum")
        eob_done = sem("eob_done")
        eow_done = sem("eow_done")
        added = sem("added")
        landed = sem("landed")
        fst_done = sem("fst_done")
        fmv_done = sem("fmv_done")
        fveps_done = sem("fveps_done")
        frstd_done = sem("frstd_done")
        fo_done = sem("fo_done")
        fnmr_done = sem("fnmr_done")
        w1_in = [sem("w1_in_even"), sem("w1_in_odd")]
        w2_in = [sem("w2_in_even"), sem("w2_in_odd")]
        xg_in = [sem("xg_in_even"), sem("xg_in_odd")]
        yt_in = [sem(f"yt_in_{s}") for s in range(NT // FT)]
        out_stored = sem("out_stored")

        def apart(eng):
            eng.nop(nofuse=True)

        SPANS = {"A": (0, NT),
                 "B": (1, NT + 1),
                 "F": (2, NT + 2),
                 "L": (LEAD - 1, NT + LEAD - 1),
                 "C": (LEAD, NT + LEAD),
                 "E": (LEAD + 1, NT + LEAD + 1),
                 "D": (BACK, NT + BACK),
                 "R": (BACK + 1, NT + BACK + 1),
                 "S": (BACK + 2, NT + BACK + 2)}

        def phases(names):
            ends = sorted({n for s in names for n in SPANS[s]} | {LEAD - 1, FULL, NT})
            return [(a, b, QT if a == FULL else 1, [s for s in names if SPANS[s][0] <= a and b <= SPANS[s][1]])
                    for a, b in zip(ends, ends[1:])]

        def tile_number(i, per, within):
            return i if per == 1 else Tile(i, within)

        def tcol(t):
            return bass.ds((t % QT) * P, P)

        block = ctx.enter_context(nc.Block())

        @block.sync
        def _(sp):
            def load_expert(e, k):
                sp.dma_start(w1_sb[k][:, :, :], w1[e].rearrange("(k p) n -> p k n", p=P)).then_inc(w1_in[k], 16)
                sp.dma_start(w2_sb[k][:, :, :], w2[e].rearrange("(g p) n -> p g n", p=P)).then_inc(w2_in[k], 16)

            sp.dma_start(x_ring[:, 0, :], x[0:P, :]).then_inc(x_loaded, 16)
            sp.dma_start(in_sb[:, :, :], in_w.rearrange("(k p) n -> p k n", p=P)).then_inc(in_proj_in, 16)
            for dst, src in ((nw_sb[:, :], norm_w),
                             (nb_sb[:, :], norm_b),
                             (cw_sb[:, :, :], conv_w.rearrange("(g p) o j -> p g (o j)", p=P)),
                             (cb_sb[:, :], conv_b),
                             (ds_sb[:, :], d_skip),
                             (dt_sb[0:1, :], dt_w),
                             (dt_sb[1:2, :], dt_b.rearrange("(o d) -> o d", o=1)),
                             (alog_sb[:, :, :], a_log.rearrange("(g p) n -> p g n", p=P)),
                             (b1_sb[:, :, :], b1),
                             (rb_sb[:, :], router_b.partition_broadcast(P))):
                sp.dma_start(dst, src).then_inc(small_in, 16)
            sp.dma_start(xp_sb[:, :, :], xp_w.rearrange("(g p) n -> p g n", p=P)).then_inc(weights_in, 16)
            sp.dma_start(out_sb[:, :, :], out_w.rearrange("(g p) n -> p g n", p=P)).then_inc(weights_in, 16)
            sp.dma_start(rw_sb[:, :, :], router_w.rearrange("(k p) n -> p k n", p=P)).then_inc(weights_in, 16)
            sp.dma_start(w1_sb[0][:, :, :], w1[0].rearrange("(k p) n -> p k n", p=P)).then_inc(w1_in[0], 16)

            for first, last, per, stages in phases("ABLDR"):
                with sp.Fori(first // per, last // per) as loop:
                    for within in range(per):
                        i = tile_number(loop, per, within)
                        t, b, c1, p, q = i, i - 1, i - LEAD + 1, i - BACK, i - BACK - 1
                        if "A" in stages:
                            if "D" in stages:
                                sp.wait_ge(r_done, past(p))
                            apart(sp)
                            sp.wait_ge(x_loaded, 16 * (t + 1))
                            sp.dma_start(x_ring[:, (t + 1) % XR, :],
                                         x.rearrange("(t p) d -> t p d", p=P)[(t + 1) % NT, :, :])\
                                .then_inc(x_loaded, 16)
                        if "L" in stages:
                            sp.wait_ge(b_stored, 16 * QT * (c1 // QT + 1) + 16)
                            apart(sp)
                            sp.wait_ge(b_loaded, 16 * c1 + 16)
                            sp.wait_ge(u_ready, STEPS * c1 + U0 - STEPS)
                            sp.dma_start(b_bc[:, c1 % 2, :, :].rearrange("p n t -> p (n t)"),
                                         b_rows.rearrange("s n t -> (s n t)")
                                         .rearrange("(c r) -> c r", r=NB * SEC)[number(c1), :]
                                         .partition_broadcast(P)).then_inc(b_loaded, 16)
                        if "R" in stages:
                            sp.wait_ge(x1_done, past(q + 1))
                            sp.dma_start(y_rows.rearrange("(t p) d -> t p d", p=P)[number(q), :, :],
                                         x1_tile[:, :]).then_inc(y_stored, 16)
                        if "B" in stages:
                            sp.wait_ge(xp_done, past(3 * (b + 1)))
                            sp.dma_start(b_rows[b // QT, :, tcol(b)], bt_tile[1:1 + NST, :]).then_inc(b_stored, 16)

            sp.wait_ge(scattered, 32 * NT + 16)
            sp.wait_ge(y_stored, 16 * NT + 16)
            for k in range(2):
                sp.dma_start(xg[:, k], slot_rows.rearrange("(e t p) c -> e p t c", p=P, t=ST)[k])\
                    .then_inc(xg_in[k], 16)
            sp.dma_start(w2_sb[0][:, :, :], w2[0].rearrange("(g p) n -> p g n", p=P)).then_inc(w2_in[0], 16)
            load_expert(1, 1)
            with sp.Fori(1, EXPERTS // 2) as pair:
                e = 2 * pair
                for k in range(2):
                    sp.wait_ge(down_psum, past(ST * (e + k - 1)))
                    sp.wait_ge(eow_done, past(ST * (e + k - 1)))
                    sp.dma_start(xg[:, k], slot_rows.rearrange("(e t p) c -> e p t c", p=P, t=ST)[e + k])\
                        .then_inc(xg_in[k], 16)
                    load_expert(e + k, k)

            y_v = y_rows.rearrange("(s t p) d -> s p t d", p=P, t=FT)
            out_v = out.rearrange("(s t p) d -> s p t d", p=P, t=FT)
            sp.wait_ge(added, 16 * ST * EXPERTS + 16)
            for s in range(NT // FT):
                sp.dma_start(yt[:, s * FT:(s + 1) * FT], y_v[s]).then_inc(yt_in[s], 16)
            for s in range(NT // FT):
                sp.wait_ge(fo_done, FT * (s + 1))
                sp.dma_start(out_v[s], yo[:, s * FT:(s + 1) * FT]).then_inc(out_stored, 16)
            sp.wait_ge(out_stored, 16 * (NT // FT))

        @block.gpsimd
        def _(pool):
            pool.memset(ident[:, :], 0.0).then_inc(masks_made, 1)
            pool.memset(upper[:, :], 1.0).then_inc(masks_made, 1)
            pool.memset(ones[:, :], 1.0).then_inc(masks_made, 1)
            pool.iota(iota8[:, :], pattern=[[1, EXPERTS]], base=0, channel_multiplier=0,
                      allow_small_or_imprecise_dtypes=True).then_inc(masks_made, 1)
            pool.iota(token_no[:, :], pattern=[[P, NT]], base=0, channel_multiplier=1,
                      allow_small_or_imprecise_dtypes=True).then_inc(masks_made, 1)
            pool.wait_ge(masks_made, 5)
            pool.affine_select(out=ident[:, :], in_=ident[:, :], compare_op=ALU.not_equal, fill=1.0, base=0,
                               pattern=[[-1, P]], channel_multiplier=1).then_inc(masks_made, 1)
            pool.affine_select(out=upper[:, :], in_=upper[:, :], compare_op=ALU.is_gt, fill=0.0, base=0,
                               pattern=[[1, P]], channel_multiplier=-1).then_inc(masks_made, 1)
            pool.memset(zero[:, :], 0.0).then_inc(state_zeroed, 1)
            pool.memset(eps[:, :], EPS).then_inc(state_zeroed, 1)
            pool.memset(rows[:, :, :], 0.0).then_inc(state_zeroed, 1)
            pool.memset(slot[:, :], SLOTS).then_inc(state_zeroed, 1)
            pool.memset(gden[:, :], 1.0).then_inc(state_zeroed, 1)
            pool.memset(gtop[:, :], 0.0).then_inc(state_zeroed, 1)
            pool.memset(mhalf[:, :], -0.5).then_inc(masks_made, 1)
            pool.memset(xp0[:, :], 1.0).then_inc(state_zeroed, 1)
            pool.memset(halo[:, :, :, :], 0.0).then_inc(state_zeroed, 1)
            pool.memset(carry[:, :, :, :], 0.0).then_inc(state_zeroed, 1)
            pool.memset(taken[:, :], 0.0).then_inc(state_zeroed, 1)
            pool.memset(acc[:, :, :, :], 0.0).then_inc(state_zeroed, 1)
            pool.wait_ge(masks_made, 8)
            pool.wait_ge(empty_made, 2)
            pool.dma_start(slot_rows.rearrange("(t p) c -> p t c", p=P),
                           empty_row[:, :].rearrange("p (a c) -> p a c", a=1).to_broadcast([P, SLOTS // P, ROW]))\
                .then_inc(scattered, 16)

            def make_u(c, k):
                j, g = k // DG, k % DG
                if k == 0:
                    pool.wait_ge(dx_done, past(QT * (c // QT) + QT))
                    pool.wait_ge(b_loaded, 16 * (c + 1) + 16)
                pool.wait_ge(scans_done, STEPS * c + k - 3 + SCAN0)
                apart(pool)
                pool.tensor_tensor(u[:, k % 4, :], dx[:, (c // QT) % 2, g, :], b_bc[:, c % 2, j, :],
                                   ALU.mult).then_inc(u_ready, 1)

            def make_delta(f, c, scanning):
                pool.wait_ge(sprelu_done, past(f + 1))
                pool.wait_ge(spln_done, number(f + 1))
                if scanning:
                    pool.wait_ge(scans_done, STEPS * QT * (c // QT) + SCAN0)
                apart(pool)
                pool.tensor_tensor(delta[:, (f // QT) % 2, :, tcol(f)], sp_ln[:, :, :], sp_relu[:, :, :],
                                   ALU.add).then_inc(delta_done, 1)

            def make_dx(f):
                pool.wait_ge(delta_done, past(f + 1))
                pool.wait_ge(xc_done, past(f + 1))
                apart(pool)
                pool.tensor_tensor(dx[:, (f // QT) % 2, :, tcol(f)], delta[:, (f // QT) % 2, :, tcol(f)],
                                   xc[:, f % RT, :, :], ALU.mult).then_inc(dx_done, 1)

            def number_rows(q):
                pool.wait_ge(scattered, 32 * q + 16)
                apart(pool)
                pool.tensor_copy(rows[:, :, DIM + 1], token_no[:, bass.ds(number(q), 1)].to_broadcast([P, 2]))\
                    .then_inc(ids_done, 1)

            def dispatch(q, k):
                if k == 0:
                    pool.wait_ge(slot_done, number(q + 1))
                    pool.wait_ge(gate_done, past(q + 1))
                    pool.wait_ge(x1_copied, past(q + 1))
                    pool.wait_ge(ids_done, number(q + 1))
                apart(pool)
                pool.indirect_dma_start(
                    slot_rows[:, :], bass.IndirectOffsetOnAxis(ap=slot[:, k:k + 1], axis=0),
                    rows[:, k, :], None, bounds_check=SLOTS - 1, oob_is_err=False).then_inc(scattered, 16)

            for first, last, per, stages in phases("FCRS"):
                with pool.Fori(first // per, last // per) as loop:
                    for within in range(per):
                        i = tile_number(loop, per, within)
                        f, c, q = i - 2, i - LEAD, i - BACK - 1
                        for k in range(STEPS):
                            if "C" in stages:
                                make_u(c, k)
                            if "S" in stages and k in (0, 2):
                                dispatch(q - 1, k // 2)
                            if "F" in stages and k == 5:
                                make_delta(f, c, "C" in stages)
                            if "F" in stages and k == 7:
                                make_dx(f)
                            if "R" in stages and k == 9:
                                number_rows(q)

            pool.wait_ge(scattered, 32 * NT + 16)
            pool.wait_ge(y_stored, 16 * NT + 16)
            pool.dma_start(b2_bc[:, :, :].rearrange("p e d -> p (e d)"),
                           b2.rearrange("e d -> (e d)").partition_broadcast(P)).then_inc(added, 16)

            def add_rows(e, k):
                pool.wait_ge(added, 16 * ST * e + 16)
                pool.sem_inc(landed, 1)
                apart(pool)
                pool.wait_ge(gidx_done, e + 1)
                for t in range(ST):
                    pool.wait_ge(eow_done, past(ST * e + t + 1))
                    apart(pool)
                    pool.indirect_dma_start(
                        y_rows[:, :], bass.IndirectOffsetOnAxis(ap=gidx[:, k, t:t + 1], axis=0), eo_w[:, k, t, :],
                        None, bounds_check=TOK - 1, oob_is_err=False, compute_op=ALU.add).then_inc(added, 16)

            with pool.Fori(0, EXPERTS // 2) as pair:
                e = 2 * pair
                for k in range(2):
                    add_rows(e + k, k)

            for s in range(NT // FT):
                now = slice(s * FT, (s + 1) * FT)
                pool.wait_ge(fmv_done, FT * (s + 1))
                pool.tensor_scalar(fveps[:, now], fmv[:, now, 1], EPS, None, ALU.add).then_inc(fveps_done, 1)
                pool.wait_ge(fveps_done, s + 1)
                pool.tensor_tensor(frstd[:, now], fveps[:, now], mhalf[:, :], ALU.pow).then_inc(frstd_done, 1)

        @block.scalar
        def _(act):
            for count, credit in ((scans_done, SCAN0), (u_ready, U0), (hT_psum, HT0), (acc_done, ACC0),
                                  (carry_saved, CARRY0), (acc_zeroed, ACCZ0), (gelu_done, GEL0), (eob_done, EOB0),
                                  (b_stored, 16), (y_stored, 16), (b_loaded, 16)):
                act.sem_inc(count, credit)
            for count in (xc_done, y_done, sz_done, yT_psum, z_psum, conv_psum, xi_done, dx_done, dt_psum, delta_done,
                          gate_done, down_psum, xp_done, pos_done, lg_done, sprelu_done, xgT_done, xnT_psum, o_psum,
                          x1_done, x1_copied, gexp_done, cnt_psum, taken_done, eow_done, landed, r_done, x1T_done,
                          x1T_psum):
                act.sem_inc(count, 1)
            act.wait_ge(small_in, 16 * 10)
            act.activation(aexp[:, :, :], alog_sb[:, :, :], ACT.Exp).then_inc(aexp_done, 1)
            act.wait_ge(aexp_done, 1)
            act.activation(nega[:, :, :].rearrange("p n g -> p g n"), aexp[:, :, :], ACT.Copy, scale=-1.0)\
                .then_inc(nega_done, 1)
            act.wait_ge(nega_done, 1)
            act.wait_ge(state_zeroed, 11)

            def decay(c, k):
                j, g = k // DG, k % DG
                if k == 0:
                    act.wait_ge(delta_done, past(QT * (c // QT) + QT))
                act.wait_ge(scans_done, STEPS * c + k - 3 + SCAN0)
                apart(act)
                act.activation(decays[k % 4], delta[:, (c // QT) % 2, g, :], ACT.Exp,
                               scale=nega[:, bass.ds((c % QT) * NB + j, 1), g]).then_inc(decay_ready, 1)

            def take_acc(p):
                act.wait_ge(acc_done, QT * NST * (p // QT) + QT * NST + ACC0)
                act.wait_ge(yT_psum, past(p))
                apart(act)
                act.activation(acc_tile[:, :], acc[:, (p // QT) % 2, p % QT, :], ACT.Copy).then_inc(acct_done, 1)

            def clear_acc(p):
                act.wait_ge(acct_done, number(p + 1))
                apart(act)
                act.activation(acc[:, (p // QT) % 2, p % QT, :], zero[:, 0:1].to_broadcast([P, DI]), ACT.Copy)\
                    .then_inc(acc_zeroed, 1)

            def front_inverse_std(t):
                act.wait_ge(mv1_done, number(t + 1))
                apart(act)
                act.activation(veps[:, 0:1], mv[:, 1:2], ACT.Ln, bias=eps[:, 0:1]).then_inc(veps1_done, 1)
                act.wait_ge(veps1_done, number(t + 1))
                act.activation(rstd[:, 0:1], veps[:, 0:1], ACT.Exp, scale=-0.5).then_inc(rstd1_done, 1)

            def back_inverse_std(p):
                act.wait_ge(mv2_done, number(p + 1))
                apart(act)
                act.activation(veps2[:, :], mv2[:, 1:2], ACT.Ln, bias=eps[:, 0:1]).then_inc(veps2_done, 1)
                act.wait_ge(veps2_done, number(p + 1))
                act.activation(rstd2[:, :], veps2[:, :], ACT.Exp, scale=-0.5).then_inc(rstd2_done, 1)

            def take_xnT(t):
                act.wait_ge(xnT_psum, past(t + 1))
                act.wait_ge(z_psum, past(t))
                for k in range(KD):
                    act.activation(xnT[:, k, :], front_a[:, k * P:(k + 1) * P], ACT.Identity,
                                   bias=nb_sb[:, k:k + 1], scale=nw_sb[:, k:k + 1]).then_inc(xnT_done, 1)

            def take_xi(t):
                act.wait_ge(xi_psum, number(t + 1))
                act.wait_ge(conv_psum, past(t))
                act.wait_ge(xi_done, past(2 * t))
                apart(act)
                act.activation(xi[:, :, 0:TAPS - 1], halo[:, t // TPB, :, :], ACT.Copy).then_inc(halo_in, 1)
                ps = front_b.rearrange("p (g t) -> p g t", g=DG)
                act.activation(xi[:, :, TAPS - 1:], ps, ACT.Copy).then_inc(xi_done, 1)
                act.wait_ge(halo_in, number(t + 1))
                apart(act)
                act.activation(halo[:, t // TPB, :, :], ps[:, :, P - TAPS + 1:P], ACT.Copy).then_inc(xi_done, 1)

            def take_z_xc(b, back, q):
                act.preload_act_table_set("silu_and_others")
                act.wait_ge(z_psum, past(b + 1))
                if back:
                    act.wait_ge(y_done, past(q + 1))
                act.activation(sz[:, b % RT, :, :], front_a.rearrange("p (g t) -> p g t", g=DG),
                               ACT.Silu).then_inc(sz_done, 1)
                act.wait_ge(conv_psum, past(b + 1))
                act.wait_ge(xc_done, past(b))
                for g in range(DG):
                    act.activation(xc_tile[:, g, :], front_b[:, g * P:(g + 1) * P], ACT.Silu,
                                   bias=cb_sb[:, g:g + 1]).then_inc(xct_done, 1)
                act.preload_act_table_set("natural_log_exp_and_others")

            def keep_xc(b, back, q):
                act.wait_ge(xct_done, DG * (b + 1))
                if back:
                    act.wait_ge(yT_psum, past(q + 1))
                act.activation(xc[:, b % RT, :, :], xc_tile[:, :, :], ACT.Copy).then_inc(xc_done, 1)

            def take_xp(t, bank):
                act.wait_ge(xp_psum, number(t + 1))
                act.wait_ge(b_stored, 16 * t + 16)
                act.activation(bt_tile[:, :], bank[0:1 + NST, 0:P], ACT.Copy).then_inc(xp_done, 1)
                act.wait_ge(dt_psum, past(t))
                act.activation(xp0[0:1, :], bank[0:1, 0:P], ACT.Copy).then_inc(xp_done, 1)
                act.activation(c_sb[:, (t // QT) % 3, t % QT, :], bank[:, P:P + NST], ACT.Copy)\
                    .then_inc(xp_done, 1)

            def softplus_part(b, n, bank):
                v = bank.rearrange("p (g t) -> p g t", g=DG)
                if n == 0:
                    act.wait_ge(dt_psum, past(b + 1))
                    act.wait_ge(delta_done, past(b))
                    act.activation(sp_ln[:, :, :], v, ACT.Abs).then_inc(spabs_done, 1)
                if n == 1:
                    act.activation(sp_relu[:, :, :], v, ACT.Relu).then_inc(sprelu_done, 1)
                if n == 2:
                    act.wait_ge(spabs_done, number(b + 1))
                    act.activation(sp_ln[:, :, :], sp_ln[:, :, :], ACT.Exp, scale=-1.0).then_inc(spexp_done, 1)
                if n == 3:
                    act.wait_ge(spexp_done, number(b + 1))
                    act.activation(sp_ln[:, :, :], sp_ln[:, :, :], ACT.Ln, bias=1.0).then_inc(spln_done, 1)

            def fill_rows(q):
                act.wait_ge(x1_done, past(q + 1))
                act.wait_ge(scattered, 32 * q + 16)
                act.activation(rows[:, :, 0:DIM],
                               x1_tile[:, :].rearrange("p (a d) -> p a d", a=1).to_broadcast([P, 2, DIM]), ACT.Copy)\
                    .then_inc(x1_copied, 1)

            def take_x1T(q):
                act.wait_ge(x1T_psum, past(q + 1))
                act.activation(x1T[:, :, :].rearrange("p k t -> p (k t)"), back_a[:, 0:KD * P], ACT.Copy)\
                    .then_inc(x1T_done, 1)

            def gate_exps(p):
                act.wait_ge(negmax_done, number(p + 1))
                act.wait_ge(gate_done, past(p))
                act.activation(gexp[:, :], logits[:, :], ACT.Exp, bias=negmax[:, 0:1], accum_out=gden[:, 0:1])\
                    .then_inc(gexp_done, 1)
                act.activation(gtop[:, :], top8[:, 0:2], ACT.Exp, bias=negmax[:, 0:1]).then_inc(gexp_done, 1)

            def fill(t, second, last):
                take_xnT(t)
                if second:
                    keep_xc(t - 1, False, t)
                    take_xp(t - 1, back_b)
                take_xi(t)
                front_inverse_std(t + 1)
                if second:
                    for n in range(4):
                        softplus_part(t - 1, n, back_a)
                if not last:
                    take_z_xc(t, False, t)

            def drain(p, q, stages):
                if "E" in stages:
                    back_inverse_std(q)
                if "D" in stages:
                    take_acc(p)
                if "R" in stages:
                    if "E" not in stages:
                        back_inverse_std(q)
                    take_x1T(q)
                    fill_rows(q)
                    gate_exps(q)

            act.preload_act_table_set("natural_log_exp_and_others")
            act.wait_ge(state_zeroed, 11)
            front_inverse_std(0)
            for first, last, per, stages in phases("ABCEDR"):
                with act.Fori(first // per, last // per) as loop:
                    for within in range(per):
                        i = tile_number(loop, per, within)
                        t, c, p, q = i, i - LEAD, i - BACK, i - BACK - 1
                        if "C" not in stages:
                            if "A" in stages:
                                fill(t, "B" in stages, last == LEAD)
                            else:
                                drain(p, q, stages)
                            continue
                        for k in range(STEPS):
                            if "C" in stages:
                                decay(c, k)
                            if "R" in stages and k == 2:
                                back_inverse_std(q)
                            if "B" in stages and k == 3:
                                take_z_xc(t - 1, "R" in stages, q)
                            if "B" in stages and k == 4:
                                keep_xc(t - 1, "R" in stages, q)
                            if "R" in stages and k == 4:
                                take_x1T(q)
                            if "R" in stages and k == 5:
                                fill_rows(q)
                            if "A" in stages and k == 6:
                                take_xnT(t)
                            if "D" in stages and k == 7:
                                take_acc(p)
                            if "R" in stages and k == 9:
                                gate_exps(q)
                            if "A" in stages and k == 9:
                                take_xi(t)
                            if "B" in stages and k == 10:
                                if "C" in stages:
                                    act.wait_ge(acc_done, QT * NST * (c // QT) + ACC0)
                                take_xp(t - 1, front_a)
                            if "D" in stages and k == 11:
                                clear_acc(p)
                            if "B" in stages and k == 12:
                                softplus_part(t - 1, 0, front_b)
                                softplus_part(t - 1, 1, front_b)
                            if "B" in stages and k in (13, 14):
                                softplus_part(t - 1, k - 11, front_b)
                            if "A" in stages and k == 14:
                                front_inverse_std(t + 1)

            def gelu(e, k):
                act.wait_ge(down_psum, past(ST * e))
                for m in range(HG):
                    act.wait_ge(up_psum, HG * e + m + 1)
                    pair = banks[:, 2 * (m % 2):2 * (m % 2) + 2, 0:HALF]
                    act.activation(hid[:, m, :].rearrange("p (a b) -> p a b", a=2), pair, ACT.Gelu,
                                   bias=b1_sb[:, e, m:m + 1]).then_inc(gelu_done, 1)

            act.preload_act_table_set("gelu_and_others")
            act.wait_ge(scattered, 32 * NT + 16)
            with act.Fori(0, EXPERTS // 2) as pair:
                e = 2 * pair
                for k in range(2):
                    gelu(e + k, k)

            for s in range(NT // FT):
                act.wait_ge(fnmr_done, s + 1)
                for n in range(s * FT, (s + 1) * FT):
                    act.activation(yo[:, n, :], yt[:, n, :], ACT.Identity,
                                   bias=nmr[:, n:n + 1], scale=frstd[:, n:n + 1]).then_inc(fo_done, 1)

        @block.tensor
        def _(pe):
            pe.wait_ge(masks_made, 8)

            def state_sums(c, k):
                j, tt = k // DG, k % DG
                if tt == 0:
                    pe.wait_ge(scans_done, STEPS * c + DG * (j + 1) + SCAN0)
                pe.wait_ge(acc_done, STEPS * c + k - 1 + ACC0)
                if k in (0, 5, 6, 7, 8, 12, 13, 14, 15):
                    pe.matmul(hT_ps[k % 2][:, 0:P], ident[:, :], ident[:, :], start=True, stop=True)
                for g in range(DG):
                    mm = pe.transpose(hT_ps[k % 2][:, g * P:(g + 1) * P], h[:, j % 2, g, tt * P:(tt + 1) * P],
                                      ident[:, :])
                mm.then_inc(hT_psum, 1)

            def x_norm_T(t):
                pe.wait_ge(xn_done, number(t + 1))
                pe.wait_ge(sz_done, past(t))
                for k in range(KD):
                    mm = pe.transpose(front_a[:, k * P:(k + 1) * P], xn[:, k * P:(k + 1) * P], ident[:, :])
                mm.then_inc(xnT_psum, 1)

            def project_in(half, bank, m):
                for k in range(KD):
                    mm = pe.matmul(bank[:, m * P:(m + 1) * P],
                                   in_sb[:, k, half * DI + m * P:half * DI + (m + 1) * P], xnT[:, k, :],
                                   start=(k == 0), stop=(k == KD - 1))
                return mm

            def convolve(g):
                for j in range(TAPS):
                    mm = pe.matmul(front_b[:, g * P:(g + 1) * P], conv_diag[:, g, j, :], xi[:, g, j:j + P],
                                   start=(j == 0), stop=(j == TAPS - 1))
                return mm

            def project_x(b, bank):
                pe.wait_ge(xct_done, DG * (b + 1))
                for g in range(DG):
                    pe.matmul(bank[0:1 + NST, 0:P], xp_sb[:, g, 0:1 + NST], xc_tile[:, g, :],
                              start=(g == 0), stop=(g == DG - 1))
                for g in range(DG):
                    mm = pe.matmul(bank[:, P:P + NST], xc_tile[:, g, :], xp_sb[:, g, 1 + NST:],
                                   start=(g == 0), stop=(g == DG - 1))
                mm.then_inc(xp_psum, 1)

            def project_dt(t, bank):
                pe.wait_ge(xp_done, past(3 * (t + 1)))
                for g in range(DG):
                    mm = pe.matmul(bank[:, g * P:(g + 1) * P], dt_sb[:, g * P:(g + 1) * P], xp0[:, :],
                                   start=True, stop=True)
                mm.then_inc(dt_psum, 1)

            def y_channels(p, g0, g1, bank):
                for g in range(g0, g1):
                    pe.matmul(bank[:, g * P:(g + 1) * P], acc_tile[:, g * P:(g + 1) * P], ident[:, :],
                              start=True, stop=False)
                    mm = pe.matmul(bank[:, g * P:(g + 1) * P], skip_diag[:, g, :],
                                   xc[:, p % RT, g, :], start=False, stop=True)
                return mm

            def project_out(p, g0, g1, bank):
                for g in range(g0, g1):
                    mm = pe.matmul(bank[:, 0:DIM], y_tile[:, g, :], out_sb[:, g, :],
                                   start=(g == 0), stop=(g == DG - 1))
                return mm

            def x1_T(p):
                pe.wait_ge(x1_done, past(p + 1))
                for k in range(KD):
                    mm = pe.transpose(back_a[:, k * P:(k + 1) * P], x1_tile[:, k * P:(k + 1) * P], ident[:, :])
                mm.then_inc(x1T_psum, 1)

            def route(p):
                pe.wait_ge(x1T_done, past(p + 1))
                pe.wait_ge(r_done, past(p + 1))
                for k in range(KD):
                    mm = pe.matmul(back_b[:, 0:EXPERTS], x1T[:, k, :], rw_sb[:, k, :],
                                   start=(k == 0), stop=(k == KD - 1))
                mm.then_inc(lg_psum, 1)

            def count(p):
                pe.wait_ge(mask_done, number(p + 1))
                pe.matmul(back_b[:, 0:EXPERTS], upper_b[:, :], mask_b[:, :], start=True, stop=True)
                pe.matmul(back_b[:, EXPERTS:2 * EXPERTS], ones_b[:, :], mask_b[:, :], start=True, stop=True)\
                    .then_inc(cnt_psum, 1)

            def fill(t, second):
                b = t - 1
                x_norm_T(t)
                if second:
                    project_x(b, back_b)
                pe.wait_ge(xnT_done, KD * (t + 1))
                if second:
                    pe.wait_ge(xct_done, DG * t)
                else:
                    pe.wait_ge(in_proj_in, 16)
                for m in range(DG):
                    mm = project_in(0, front_b, m)
                mm.then_inc(xi_psum, 1)
                if second:
                    pe.wait_ge(sprelu_done, past(b))
                    project_dt(b, back_a)
                for m in range(DG):
                    mm = project_in(1, front_a, m)
                mm.then_inc(z_psum, 1)
                pe.wait_ge(xi_done, past(2 * (t + 1)))
                if not second:
                    pe.wait_ge(weights_in, 16 * 3)
                    pe.wait_ge(small_in, 16 * 10)
                    pe.wait_ge(consts_made, 2 + DG * TAPS + DG)
                    pe.wait_ge(state_zeroed, 11)
                for g in range(DG):
                    mm = convolve(g)
                mm.then_inc(conv_psum, 1)

            def drain(p, q, stages):
                if "D" in stages:
                    pe.wait_ge(acct_done, number(p + 1))
                    pe.wait_ge(y_done, past(p))
                    y_channels(p, 0, DG, front_a).then_inc(yT_psum, 1)
                if "R" in stages and "E" not in stages:
                    x1_T(q)
                if "R" in stages:
                    pe.wait_ge(pos_done, past(2 * q))
                    route(q)
                if "D" in stages:
                    pe.wait_ge(y_done, past(p + 1))
                    pe.wait_ge(r_done, past(p))
                    project_out(p, 0, DG, front_b).then_inc(o_psum, 1)
                if "R" in stages:
                    count(q)

            for first, last, per, stages in phases("ABCEDR"):
                with pe.Fori(first // per, last // per) as loop:
                    for within in range(per):
                        i = tile_number(loop, per, within)
                        t, b, c, p, q = i, i - 1, i - LEAD, i - BACK, i - BACK - 1
                        if "C" not in stages:
                            if "A" in stages:
                                fill(t, "B" in stages)
                            else:
                                drain(p, q, stages)
                            continue
                        for k in range(STEPS):
                            if "C" in stages:
                                state_sums(c, k)
                            if "A" in stages and k == 0:
                                x_norm_T(t)
                            if "R" in stages and k == 0:
                                route(q)
                            if "A" in stages and k == 1:
                                pe.wait_ge(xnT_done, KD * (t + 1))
                                pe.wait_ge(xct_done, DG * t)
                                project_in(0, front_b, 0)
                                project_in(0, front_b, 1)
                            if "A" in stages and k == 2:
                                project_in(0, front_b, 2)
                                project_in(0, front_b, 3).then_inc(xi_psum, 1)
                            if "D" in stages and k == 3:
                                pe.wait_ge(acct_done, number(p + 1))
                                pe.wait_ge(x1T_done, past(p))
                                y_channels(p, 0, 2, back_a)
                            if "D" in stages and k == 3:
                                y_channels(p, 2, DG, back_a).then_inc(yT_psum, 1)
                            if "R" in stages and k == 5:
                                count(q)
                            if "B" in stages and k == 4:
                                if "A" in stages:
                                    pe.wait_ge(xnT_done, KD * (t + 1))
                                project_x(b, front_a)
                            if "B" in stages and k == 6:
                                if "A" in stages:
                                    pe.wait_ge(xi_done, past(2 * (t + 1)))
                                project_dt(b, front_b)
                            if "D" in stages and k == 7:
                                pe.wait_ge(y_done, past(p + 1))
                                pe.wait_ge(pos_done, past(2 * p))
                                project_out(p, 0, 2, back_b)
                            if "D" in stages and k == 8:
                                project_out(p, 2, DG, back_b).then_inc(o_psum, 1)
                            if "A" in stages and k == 9:
                                pe.wait_ge(xi_done, past(2 * (t + 1)))
                                pe.wait_ge(sprelu_done, past(b + 1))
                                convolve(0)
                            if "A" in stages and k == 9:
                                convolve(1)
                            if "A" in stages and k == 10:
                                convolve(2)
                            if "A" in stages and k == 10:
                                convolve(3).then_inc(conv_psum, 1)
                            if "A" in stages and k == 11:
                                pe.wait_ge(xp_done, past(3 * (b + 1)))
                                project_in(1, front_a, 0)
                            if "A" in stages and k == 11:
                                project_in(1, front_a, 1)
                            if "A" in stages and k == 12:
                                project_in(1, front_a, 2)
                            if "A" in stages and k == 12:
                                project_in(1, front_a, 3).then_inc(z_psum, 1)
                            if "D" in stages and k == 13:
                                x1_T(p)

            def gathered_T(e, k, kd):
                if kd == 0:
                    pe.wait_ge(xg_in[k], 8 * (e - k) + 16)
                pe.wait_ge(xgT_done, past(KD * e + kd))
                for t in range(ST):
                    mm = pe.transpose(banks[:, 6:8, :].rearrange("p a b -> p (a b)")[:, t * P:(t + 1) * P],
                                      xg[:, k, t, kd * P:(kd + 1) * P], ident[:, :])
                mm.then_inc(xgT_psum, 1)

            def expert(e, k, following):
                pe.wait_ge(w1_in[k], 8 * (e - k) + 16)
                pe.wait_ge(xgT_done, past(KD * (e + 1)))
                for m in range(HG):
                    pe.wait_ge(gelu_done, HG * e + m - 1 + GEL0)
                    for a in range(2):
                        for kd in range(KD):
                            mm = pe.matmul(banks[:, 2 * (m % 2) + a, 0:HALF], w1_sb[k][:, kd, m * P:(m + 1) * P],
                                           xgT[:, k, kd, a * HALF:(a + 1) * HALF],
                                           start=(kd == 0), stop=(kd == KD - 1))
                    mm.then_inc(up_psum, 1)
                    if following and m in (3, 7):
                        gathered_T(e + 1, 1 - k, m // 4)
                pe.wait_ge(gelu_done, HG * (e + 1) + GEL0)
                pe.wait_ge(w2_in[k], 8 * (e - k) + 16)
                for t in range(ST):
                    pe.wait_ge(eob_done, ST * e + t - 1 + EOB0)
                    for m in range(HG):
                        mm = pe.matmul(banks[:, 4 + (ST * k + t) % 2, 0:DIM], hid[:, m, t * P:(t + 1) * P],
                                       w2_sb[k][:, m, :], start=(m == 0), stop=(m == HG - 1))
                    mm.then_inc(down_psum, 1)

            pe.wait_ge(scattered, 32 * NT + 16)
            gathered_T(0, 0, 0)
            gathered_T(0, 0, 1)
            with pe.Fori(0, EXPERTS // 2 - 1) as pair:
                e = 2 * pair
                expert(e, 0, True)
                expert(e + 1, 1, True)
            expert(EXPERTS - 2, 0, True)
            expert(EXPERTS - 1, 1, False)

        @block.vector
        def _(dve):
            def scan_step(c, k):
                j, g = k // DG, k % DG
                if g == 0:
                    dve.wait_ge(carry_saved, NB * c + j - 1 + CARRY0)
                dve.wait_ge(decay_ready, STEPS * c + k + 1)
                dve.wait_ge(u_ready, STEPS * c + k + 1 + U0)
                if g == 0:
                    dve.wait_ge(hT_psum, DG * (NB * c + j) - 4 + HT0)
                dve.tensor_tensor_scan(h[:, j % 2, g, :], decays[k % 4], u[:, k % 4, :],
                                       carry[:, c // TPB, bass.ds((c % QT) * NB + j, 1), g],
                                       ALU.mult, ALU.add).then_inc(scans_done, 1)

            def save_carry(c, j):
                dve.wait_ge(scans_done, STEPS * c + DG * (j + 1) + SCAN0)
                apart(dve)
                dve.tensor_copy(carry[:, c // TPB, bass.ds((c % QT) * NB + j, 1), :]
                                .rearrange("p a g -> p (a g)"), h[:, j % 2, :, SEC - 1])\
                    .then_inc(carry_saved, 1)

            def add_state(c, k):
                j, tt = k // DG, k % DG
                n = STEPS * c + k
                if k == 0:
                    dve.wait_ge(acc_zeroed, QT * (c // QT) - QT + ACCZ0)
                    dve.wait_ge(xp_done, past(3 * QT * (c // QT) + 3 * QT))
                dve.wait_ge(hT_psum, n + 1 + HT0)
                dve.wait_ge(acc_done, n - 3 + ACC0)
                a = acc[:, (c // QT) % 2, tt, :]
                dve.scalar_tensor_tensor(out=a, in0=hT_ps[tt % 2],
                                         scalar=c_sb[:, (c // QT) % 3, tt, bass.ds((c % QT) * NB + j, 1)],
                                         in1=a, op0=ALU.mult, op1=ALU.add).then_inc(acc_done, 1)

            def front_stats(t):
                dve.wait_ge(x_loaded, 16 * (t + 1))
                dve.bn_stats(stat[:, :], x_ring[:, t % XR, :]).then_inc(st1_done, 1)

            def front_mean(t):
                dve.wait_ge(st1_done, number(t + 1))
                apart(dve)
                dve.bn_aggr(mv[:, :], stat[:, :]).then_inc(mv1_done, 1)

            def front_norm(t):
                dve.wait_ge(rstd1_done, number(t + 1))
                dve.wait_ge(xnT_psum, past(t))
                dve.tensor_scalar(xn[:, :], x_ring[:, t % XR, :], mv[:, 0:1], rstd[:, 0:1],
                                  ALU.subtract, ALU.mult).then_inc(xn_done, 1)

            def gate_y(p, bank):
                dve.wait_ge(yT_psum, past(p + 1))
                dve.wait_ge(o_psum, past(p))
                dve.tensor_tensor(y_tile[:, :, :], bank.rearrange("p (g t) -> p g t", g=DG),
                                  sz[:, p % RT, :, :], ALU.mult).then_inc(y_done, 1)

            def residual(p, bank):
                dve.wait_ge(o_psum, past(p + 1))
                dve.wait_ge(x1_done, past(p))
                dve.scalar_tensor_tensor(out=r_tile[:, :], in0=x_ring[:, p % XR, :], scalar=2.0,
                                         in1=bank[:, 0:DIM], op0=ALU.mult, op1=ALU.add)\
                    .then_inc(r_done, 1)

            def residual_stats(p):
                dve.wait_ge(r_done, past(p + 1))
                dve.bn_stats(stat2[:, :], r_tile[:, :]).then_inc(st2_done, 1)

            def residual_mean(p):
                dve.wait_ge(st2_done, number(p + 1))
                apart(dve)
                dve.bn_aggr(mv2[:, :], stat2[:, :]).then_inc(mv2_done, 1)

            def norm_x1(p):
                dve.wait_ge(rstd2_done, number(p + 1))
                dve.wait_ge(y_stored, 16 * p + 16)
                dve.wait_ge(x1_copied, past(p))
                dve.wait_ge(x1T_psum, past(p))
                dve.tensor_scalar(x1_tile[:, :], r_tile[:, :], mv2[:, 0:1], rstd2[:, 0:1],
                                  ALU.subtract, ALU.mult).then_inc(x1_done, 1)

            def choose(q, part):
                if part == 0:
                    dve.wait_ge(lg_psum, number(q + 1))
                    dve.wait_ge(gexp_done, past(2 * q))
                    dve.tensor_tensor(logits[:, :], back_b[:, 0:EXPERTS], rb_sb[:, :], ALU.add)\
                        .then_inc(lg_done, 1)
                if part == 1:
                    dve.wait_ge(lg_done, past(q + 1))
                    apart(dve)
                    dve.max(top8[:, :], logits[:, :]).then_inc(top_done, 1)
                if part == 2:
                    dve.wait_ge(top_done, number(q + 1))
                    apart(dve)
                    dve.max_index(idx8[:, :], top8[:, :], logits[:, :]).then_inc(idx_done, 1)
                    dve.tensor_scalar(negmax[:, :], top8[:, 0:1], -1.0, None, ALU.mult).then_inc(negmax_done, 1)
                if part == 3:
                    dve.wait_ge(idx_done, number(q + 1))
                    dve.tensor_copy(idxf[:, :], idx8[:, 0:2]).then_inc(idxf_done, 1)
                if part == 4:
                    dve.wait_ge(idxf_done, number(q + 1))
                    dve.tensor_tensor(choice[:, :, :],
                                      iota8[:, :].rearrange("p (a e) -> p a e", a=1).to_broadcast([P, 2, EXPERTS]),
                                      idxf[:, :].rearrange("p (k a) -> p k a", a=1).to_broadcast([P, 2, EXPERTS]),
                                      ALU.is_equal).then_inc(choice_done, 1)
                if part == 5:
                    dve.wait_ge(choice_done, number(q + 1))
                    dve.wait_ge(cnt_psum, past(q))
                    dve.tensor_tensor(mask_b[:, :], choice[:, 0, :], choice[:, 1, :], ALU.add)\
                        .then_inc(mask_done, 1)

            def gate_weights(q, part):
                if part == 0:
                    dve.wait_ge(gexp_done, past(2 * q + 2))
                    dve.reciprocal(grec[:, :], gden[:, :]).then_inc(grec_done, 1)
                if part == 1:
                    dve.wait_ge(grec_done, number(q + 1))
                    dve.wait_ge(scattered, 32 * q + 16)
                    dve.tensor_scalar(rows[:, :, DIM], gtop[:, :], grec[:, 0:1], None, ALU.mult)\
                        .then_inc(gate_done, 1)

            def place(q, part):
                if part == 0:
                    dve.wait_ge(cnt_psum, past(q + 1))
                    dve.wait_ge(taken_done, past(q))
                    dve.tensor_tensor(pos[:, :], back_b[:, 0:EXPERTS], taken[:, :], ALU.add)\
                        .then_inc(pos_done, 1)
                if part == 1:
                    dve.wait_ge(pos_done, past(2 * q + 1))
                    dve.tensor_tensor(taken[:, :], back_b[:, EXPERTS:2 * EXPERTS], taken[:, :], ALU.add)\
                        .then_inc(pos_done, 1)
                if part == 2:
                    dve.wait_ge(pos_done, past(2 * q + 2))
                    dve.tensor_tensor(pick[:, :, :], choice[:, :, :],
                                      pos[:, :].rearrange("p (a e) -> p a e", a=1).to_broadcast([P, 2, EXPERTS]),
                                      ALU.mult).then_inc(taken_done, 1)
                if part == 3:
                    dve.wait_ge(taken_done, past(q + 1))
                    dve.tensor_reduce(posk[:, :], pick[:, :, :], mybir.AxisListType.X, ALU.add)\
                        .then_inc(pick_done, 1)
                if part == 4:
                    dve.wait_ge(pick_done, number(q + 1))
                    dve.scalar_tensor_tensor(out=slotf[:, :], in0=idxf[:, :], scalar=float(CAP), in1=posk[:, :],
                                             op0=ALU.mult, op1=ALU.add).then_inc(slotf_done, 1)
                    dve.tensor_scalar(over[:, :], posk[:, :], float(CAP), FAR, ALU.is_ge, ALU.mult)\
                        .then_inc(over_done, 1)
                if part == 5:
                    dve.wait_ge(slotf_done, number(q + 1))
                    dve.wait_ge(over_done, number(q + 1))
                    dve.wait_ge(scattered, 32 * q + 16)
                    dve.tensor_tensor(slot[:, :], slotf[:, :], over[:, :], ALU.add).then_inc(slot_done, 1)

            dve.memset(empty_row[:, 0:ROW - 1], 0.0).then_inc(empty_made, 1)
            dve.memset(empty_row[:, ROW - 1:ROW], FAR).then_inc(empty_made, 1)
            front_stats(0)
            front_mean(0)
            dve.wait_ge(masks_made, 8)
            dve.wait_ge(small_in, 16 * 10)
            dve.tensor_copy(ones_b[:, :], ones[:, :]).then_inc(consts_made, 1)
            dve.tensor_copy(upper_b[:, :], upper[:, :]).then_inc(consts_made, 1)
            for g in range(DG):
                for j in range(TAPS):
                    dve.tensor_scalar(conv_diag[:, g, j, :], ident[:, :], cw_sb[:, g, j:j + 1], None, ALU.mult)\
                        .then_inc(consts_made, 1)
            for g in range(DG):
                dve.tensor_scalar(skip_diag[:, g, :], ident[:, :], ds_sb[:, g:g + 1], None, ALU.mult)\
                    .then_inc(consts_made, 1)
            dve.wait_ge(state_zeroed, 11)

            def drain(c, p, q, stages):
                if "E" in stages:
                    add_state(c - 1, STEPS - LAG)
                if "R" in stages:
                    norm_x1(q)
                if "E" in stages:
                    for n in range(STEPS - LAG + 1, STEPS):
                        add_state(c - 1, n)
                if "D" in stages:
                    gate_y(p, front_a)
                if "R" in stages:
                    for part in range(6):
                        choose(q, part)
                if "D" in stages:
                    residual(p, front_b)
                    residual_stats(p)
                    residual_mean(p)
                if "R" in stages:
                    for part in range(6):
                        place(q, part)
                    gate_weights(q, 0)
                    gate_weights(q, 1)

            for first, last, per, stages in phases("ACEDR"):
                with dve.Fori(first // per, last // per) as loop:
                    for within in range(per):
                        i = tile_number(loop, per, within)
                        t, c, p, q = i, i - LEAD, i - BACK, i - BACK - 1
                        if "C" not in stages and "A" not in stages:
                            drain(c, p, q, stages)
                            continue
                        for k in range(STEPS):
                            if "C" in stages:
                                scan_step(c, k)
                            if "R" in stages and k == 1:
                                norm_x1(q)
                            if "A" in stages and k == 1:
                                front_norm(t)
                            if "R" in stages and k in (6, 7, 8):
                                choose(q, 2 * (k - 6))
                            if "D" in stages and k == 9:
                                gate_y(p, back_a)
                            if "R" in stages and k in (10, 11, 12):
                                place(q, 2 * (k - 10))
                            if "A" in stages and k == 11:
                                front_stats(t + 1)
                            if "D" in stages and k == 14:
                                residual_stats(p)

                            if "E" in stages and k < LAG:
                                add_state(c - 1, k + STEPS - LAG)
                            if "C" in stages and k >= LAG:
                                add_state(c, k - LAG)
                            if "E" in stages and k == 0:
                                save_carry(c - 1, NB - 1)
                            if "C" in stages and k >= DG and k % DG == 0:
                                save_carry(c, k // DG - 1)
                            if "R" in stages and k in (6, 7, 8):
                                choose(q, 2 * (k - 6) + 1)
                            if "R" in stages and k == 9:
                                gate_weights(q, 0)
                            if "R" in stages and k in (10, 11, 12):
                                place(q, 2 * (k - 10) + 1)
                            if "R" in stages and k == 10:
                                gate_weights(q, 1)
                            if "A" in stages and k == 11:
                                front_mean(t + 1)
                            if "D" in stages and k == 13:
                                residual(p, back_b)
                            if "D" in stages and k == 14:
                                residual_mean(p)

            def take_gathered(e, k):
                dve.wait_ge(xg_in[k], 8 * (e - k) + 16)
                dve.wait_ge(landed, past(e))
                dve.tensor_copy(gidx[:, k, :], xg[:, k, :, ROW - 1]).then_inc(gidx_done, 1)
                for kd in range(KD):
                    dve.wait_ge(xgT_psum, KD * e + kd + 1)
                    dve.tensor_copy(xgT[:, k, kd, :],
                                    banks[:, 6:8, :].rearrange("p a b -> p (a b)")[:, 0:CAP])\
                        .then_inc(xgT_done, 1)

            def weigh(e, k, following):
                if following:
                    take_gathered(e + 1, 1 - k)
                dve.wait_ge(landed, past(e))
                dve.wait_ge(eow_done, past(ST * e))
                for t in range(ST):
                    dve.wait_ge(down_psum, past(ST * e + t + 1))
                    dve.tensor_tensor(eo[:, t, :], banks[:, 4 + (ST * k + t) % 2, 0:DIM], b2_bc[:, e, :],
                                      ALU.add).then_inc(eob_done, 1)
                    dve.wait_ge(eob_done, ST * e + t + 1 + EOB0)
                    dve.tensor_scalar(eo_w[:, k, t, :], eo[:, t, :], xg[:, k, t, DIM:DIM + 1], None, ALU.mult)\
                        .then_inc(eow_done, 1)

            take_gathered(0, 0)
            dve.wait_ge(added, 16)
            with dve.Fori(0, EXPERTS // 2 - 1) as pair:
                e = 2 * pair
                weigh(e, 0, True)
                weigh(e + 1, 1, True)
            weigh(EXPERTS - 2, 0, True)
            weigh(EXPERTS - 1, 1, False)

            def minus_mean_rstd(s):
                now = slice(s * FT, (s + 1) * FT)
                dve.wait_ge(frstd_done, s + 1)
                dve.scalar_tensor_tensor(out=nmr[:, now], in0=fmv[:, now, 0], scalar=-1.0, in1=frstd[:, now],
                                         op0=ALU.mult, op1=ALU.mult).then_inc(fnmr_done, 1)

            for s in range(NT // FT):
                dve.wait_ge(yt_in[s], 16)
                for n in range(s * FT, (s + 1) * FT):
                    dve.bn_stats(fstat[:, n, :], yt[:, n, :]).then_inc(fst_done, 1)
                for n in range(s * FT, (s + 1) * FT):
                    dve.wait_ge(fst_done, n + 1)
                    dve.bn_aggr(fmv[:, n, :], fstat[:, n, :]).then_inc(fmv_done, 1)
                if s:
                    minus_mean_rstd(s - 1)
            minus_mean_rstd(NT // FT - 1)


_INS = ["x", "norm_w", "norm_b", "in_proj_w", "conv_w", "conv_b", "x_proj_w", "dt_w", "dt_b", "A_log", "D_skip",
        "out_proj_w", "router_w", "router_b", "w1", "b1", "w2", "b2"]


def kernel(**inputs):
    import numpy as _np
    import concourse.bacc as _bacc
    from concourse import mybir as _mybir
    from concourse.bass_utils import run_bass_kernel_spmd as _run

    nc = _bacc.Bacc("TRN2", target_bir_lowering=False, num_devices=1)
    arrays, args = {}, []
    for name in _INS:
        part = "L0_ffn_" if name in ("router_w", "router_b", "w1", "b1", "w2", "b2") else "L0_attn_"
        a = _np.asarray(inputs[part + name])
        if name == "x":
            a = a.reshape(-1, a.shape[-1])
        if name in ("in_proj_w", "x_proj_w", "out_proj_w"):
            a = a.T
        if name in ("norm_w", "norm_b", "conv_b", "D_skip"):
            a = a.reshape(-1, P).T
        if name == "dt_w":
            a = a.T
        if name == "b1":
            a = a.reshape(EXPERTS, HG, P).transpose(2, 0, 1)
        a = _np.ascontiguousarray(a)
        arrays[f"in_{name}_dram"] = a
        args.append(nc.dram_tensor(f"in_{name}_dram", a.shape, _mybir.dt.from_np(a.dtype), kind="ExternalInput").ap())
    out = nc.dram_tensor("out_0_dram", (TOK, DIM), F32, kind="ExternalOutput").ap()
    build(nc, *args, out)
    r = _run(nc, [arrays], core_ids=[0])
    return r.results[0]["out_0_dram"].reshape(BATCH, SEQ, DIM)
```
